# Optimizing a Trainium2 kernel written in Bass

```python
import numpy as np
import jax
import jax.numpy as jnp

def _softmax(x, axis=-1):
    return jax.nn.softmax(x, axis=axis)

def _gelu(x):
    return jax.nn.gelu(x, approximate=True)

def _silu(x):
    return jax.nn.silu(x)

def _sigmoid(x):
    return jax.nn.sigmoid(x)

def _layernorm(x, axis=-1, eps=1e-05):
    m = jnp.mean(x, axis=axis, keepdims=True)
    v = jnp.var(x, axis=axis, keepdims=True)
    return (x - m) / jnp.sqrt(v + eps)

def _scatter_add(tgt, idx, src, axis=0):
    return tgt.at[idx].add(src)

def _segment_sum(src, seg, n):
    return jax.ops.segment_sum(src, seg, n)
kernel_name = 'mk_xattn_ffn_d1_seqx_r2_544798'

def setup_inputs(seed: int=0):
    np.random.seed(seed)
    _w = jnp.asarray

    def _rec_inputs():
        import jax
        import jax.numpy as jnp
        _rk = jax.random.key(seed)
        x = -0.0003929 + 0.9999 * jax.random.normal(jax.random.fold_in(_rk, 1), (16, 256, 2048), jnp.float32)
        _lenS = 256 - jax.random.randint(jax.random.fold_in(_rk, 7), (16,), 0, max(1, 256 // 4) + 1, jnp.int32)
        _lenS2 = 256 - jax.random.randint(jax.random.fold_in(_rk, 8), (16,), 0, max(1, 256 // 4) + 1, jnp.int32)
        _ctx_4096P = jax.random.normal(jax.random.fold_in(_rk, 11), (16, 16, 2048), jnp.float32)
        _ctx_4096c = jax.random.dirichlet(jax.random.fold_in(_rk, 511), 0.3 * jnp.ones((16,), jnp.float32), (16, 256))
        _ctx_4096t = jnp.einsum('bsk,bkd->bsd', _ctx_4096c, _ctx_4096P)
        _ctx_4096t = _ctx_4096t * jax.lax.rsqrt(jnp.mean(jnp.square(_ctx_4096t)) + 1e-12) * 0.953939
        ctx_4096 = 2.81802e-05 + 1.00001 * (_ctx_4096t + 0.3 * jax.random.normal(jax.random.fold_in(_rk, 611), (16, 256, 2048), jnp.float32))
        return (x, ctx_4096)
    x, ctx_4096 = _rec_inputs()

    def _L0_xattn_setup():
        import jax, jax.numpy as jnp
        import numpy as np
        DIM = 256
        HEADS = 8
        DIM_HEAD = 64
        HIDDEN = HEADS * DIM_HEAD
        SCALE = DIM_HEAD ** (-0.5)
        key = jax.random.key(seed)
        ks = jax.random.split(key, 9)
        b, n = (8, 2048)
        std = 1.0 / np.sqrt(DIM)
        return {'q': jax.random.normal(ks[0], (b, DIM, n), jnp.float32), 'k': jax.random.normal(ks[1], (b, DIM, n), jnp.float32), 'v': jax.random.normal(ks[2], (b, DIM, n), jnp.float32), 'Wq': jax.random.normal(ks[3], (HIDDEN, DIM), jnp.float32) * std, 'Wk': jax.random.normal(ks[4], (HIDDEN, DIM), jnp.float32) * std, 'Wv': jax.random.normal(ks[5], (HIDDEN, DIM), jnp.float32) * std, 'Wo': jax.random.normal(ks[6], (DIM, HIDDEN), jnp.float32) * (1.0 / np.sqrt(HIDDEN)), 'bo': jax.random.normal(ks[7], (DIM,), jnp.float32) * 0.01, 'g': jnp.ones((1, DIM, 1), jnp.float32)}
    _L0_xattn_all = _L0_xattn_setup()
    _L0_xattn_in = {k: v for k, v in _L0_xattn_all.items() if k in ('Wq', 'Wk', 'Wv', 'Wo', 'bo', 'g')}
    del _L0_xattn_all

    def _L0_ffn_setup():
        import jax, jax.numpy as jnp
        import numpy as np
        N_EXPERTS = 8
        TOP_K = 2
        D_MODEL = 2048
        RANK = 64
        key = jax.random.key(seed)
        k0, k1, k2, k3 = jax.random.split(key, 4)
        inputs = jax.random.normal(k0, (4, 1024, D_MODEL), dtype=jnp.float32)
        gate_w = jax.random.normal(k1, (N_EXPERTS, D_MODEL), dtype=jnp.float32) * 0.02
        lora_A = jax.random.normal(k2, (N_EXPERTS, RANK, D_MODEL), dtype=jnp.float32) * 0.02
        lora_B = jax.random.normal(k3, (N_EXPERTS, D_MODEL, RANK), dtype=jnp.float32) * 0.02
        return {'inputs': inputs, 'gate_w': gate_w, 'lora_A': lora_A, 'lora_B': lora_B}
    _L0_ffn_all = _L0_ffn_setup()
    _L0_ffn_in = {k: v for k, v in _L0_ffn_all.items() if k in ('gate_w', 'lora_A', 'lora_B')}
    del _L0_ffn_all
    return {'x': x, 'ctx_4096': ctx_4096, 'L0_xattn_Wq': _L0_xattn_in['Wq'], 'L0_xattn_Wk': _L0_xattn_in['Wk'], 'L0_xattn_Wv': _L0_xattn_in['Wv'], 'L0_xattn_Wo': _L0_xattn_in['Wo'], 'L0_xattn_bo': _L0_xattn_in['bo'], 'L0_xattn_g': _L0_xattn_in['g'], 'L0_ffn_gate_w': _L0_ffn_in['gate_w'], 'L0_ffn_lora_A': _L0_ffn_in['lora_A'], 'L0_ffn_lora_B': _L0_ffn_in['lora_B']}

def reference(x, ctx_4096, L0_xattn_Wq, L0_xattn_Wk, L0_xattn_Wv, L0_xattn_Wo, L0_xattn_bo, L0_xattn_g, L0_ffn_gate_w, L0_ffn_lora_A, L0_ffn_lora_B):
    import jax
    import jax.numpy as jnp

    def _L0_xattn_ref(q, k, v, Wq, Wk, Wv, Wo, bo, g):
        import jax, jax.numpy as jnp
        import numpy as np
        DIM = 256
        HEADS = 8
        DIM_HEAD = 64
        HIDDEN = HEADS * DIM_HEAD
        SCALE = DIM_HEAD ** (-0.5)
        b = q.shape[0]
        qh = jnp.einsum('bcn,oc->bon', q, Wq).reshape(b, HEADS, DIM_HEAD, -1)
        kh = jnp.einsum('bcn,oc->bon', k, Wk).reshape(b, HEADS, DIM_HEAD, -1)
        vh = jnp.einsum('bcn,oc->bon', v, Wv).reshape(b, HEADS, DIM_HEAD, -1)
        qh = jax.nn.softmax(qh, axis=-2) * SCALE
        kh = jax.nn.softmax(kh, axis=-1)
        context = jnp.einsum('bhdn,bhen->bhde', kh, vh)
        out = jnp.einsum('bhde,bhdn->bhen', context, qh)
        out = out.reshape(b, HIDDEN, -1)
        out = jnp.einsum('bcn,oc->bon', out, Wo) + bo[None, :, None]
        norm = jnp.maximum(jnp.sqrt(jnp.sum(out * out, axis=1, keepdims=True)), 1e-12)
        return out / norm * g * np.sqrt(DIM)

    def _L0_ffn_ref(inputs, gate_w, lora_A, lora_B):
        import jax, jax.numpy as jnp
        import numpy as np
        N_EXPERTS = 8
        TOP_K = 2
        D_MODEL = 2048
        RANK = 64
        x = inputs.reshape(-1, inputs.shape[-1])
        T = x.shape[0]
        gate_probs = jax.nn.softmax(x @ gate_w.T, axis=-1)
        weights, sel = jax.lax.top_k(gate_probs, TOP_K)
        weights = weights / jnp.sum(weights, axis=-1, keepdims=True)
        w_full = jnp.zeros((T, N_EXPERTS), dtype=x.dtype).at[jnp.arange(T)[:, None], sel].add(weights)
        out = jnp.zeros((T, D_MODEL), dtype=x.dtype)
        for e in range(N_EXPERTS):
            y = x @ lora_A[e].T @ lora_B[e].T
            out = out + w_full[:, e:e + 1] * y
        return out.reshape(inputs.shape[:-1] + (D_MODEL,))
    x = x + _L0_xattn_ref(_layernorm(x, axis=-1), ctx_4096, ctx_4096, L0_xattn_Wq, L0_xattn_Wk, L0_xattn_Wv, L0_xattn_Wo, L0_xattn_bo, L0_xattn_g)
    x = x + _L0_ffn_ref(_layernorm(x, axis=-1), L0_ffn_gate_w, L0_ffn_lora_A, L0_ffn_lora_B)
    return x

_drawn_inputs = setup_inputs


def setup_inputs(seed=0):
    import zlib

    import numpy as np

    out = dict(_drawn_inputs(seed))
    spreads = {'L0_xattn_g': (1.0, 0.2)}
    factors = {}
    for name, (base, spread) in spreads.items():
        noise = np.random.default_rng([zlib.crc32(name.encode()), seed]).standard_normal(out[name].shape)
        drawn = base * np.exp(spread * noise) if base else spread * noise
        out[name] = jnp.asarray(drawn.astype(out[name].dtype))
    for name, factor in factors.items():
        out[name] = (out[name] * factor).astype(out[name].dtype)
    return out
```

```python
from contextlib import ExitStack

import concourse.bass as bass
from concourse import mybir

F32, F16, BF16, U32 = mybir.dt.float32, mybir.dt.float16, mybir.dt.bfloat16, mybir.dt.uint32
ALU = mybir.AluOpType
ACT = mybir.ActivationFunctionType
X = mybir.AxisListType.X

P = 128
HI, LO = 0, 1
HEADS, DH, E_N = 8, 64, 8

S_Z = 2.0**8
S_W = 2.0**6
S_C = 2.0**4
S_K = 2.0**12
S_M = 2.0**8
S_Q = 2.0**10
S_H = 2.0**5
S_N = 2.0**20

LN_EPS = 1e-5
NORM_FLOOR = 1e-12

RING = [3, 0, 4, 5]
PAIR = [1, 2]
GATE_BANK = 3
KC_BANK = [4, 5]
KT_LAG = 7
Q_LAG = 4


class Turn:

    def __init__(self, reg, off):
        self.reg, self.off = reg, off

    def at(self, per, k):
        const = self.off * per + k
        return const if self.reg is None else self.reg * per + const

    @property
    def index(self):
        return self.off if self.reg is None else self.reg + self.off

    @property
    def next(self):
        return Turn(self.reg, self.off + 1)


def build(nc, x, ctx, wqT, wkT, wvT, woT, bo, g, gateT, aT, bT, out):
    B, DIM, N = x.shape
    HID = HEADS * DH
    CC = DIM // P
    HC = HID // P
    NB = N // 512
    NT = N // P
    KTILES = HC * NB
    GROUPS = NT // 2
    assert (B, DIM, N, HID) == (16, 256, 2048, 512)

    x_v = x.rearrange("b (c p) n -> b p c n", p=P)
    c_v = ctx.rearrange("b (c p) n -> b p c n", p=P)
    o_v = out.rearrange("b (c p) n -> b p c n", p=P)

    es = ExitStack()
    with es:
        def sb(name, shape, dt):
            return es.enter_context(nc.sbuf_tensor(name, shape, dt))

        def sem(name):
            return es.enter_context(nc.semaphore(name))

        wq = sb("wq", [P, 2, CC, HID], F16)
        wk = sb("wk", [P, 2, CC, HID], F16)
        wv = sb("wv", [P, 2, CC, HID], F16)
        wo = sb("wo", [P, 2, HC, DIM], F16)
        wa = sb("wa", [P, 2, NT, HID], F16)
        wb = sb("wb", [P, 2, HC, N], F16)
        wg = sb("wg", [P, 2, NT, E_N], F16)
        wg_raw = sb("wg_raw", [P, NT, E_N], F32)
        ones = sb("ones", [P, P], F32)
        ident = sb("ident", [P, P], F32)
        ident16 = sb("ident16", [P, P], F16)
        minus1 = sb("minus1", [P, P], BF16)
        pairmask = sb("pairmask", [P, P], F32)
        experts = sb("experts", [P, E_N], F32)
        minus_half = sb("minus_half", [P, CC], F32)
        bo_c = sb("bo_c", [P, CC], F32)
        g_c = sb("g_c", [P, CC], F32)

        stage = sb("stage", [P, CC, N], F32)
        xres = sb("xres", [P, CC, N], F32)
        opnd = sb("opnd", [P, 2, CC, N], F16)
        ct_m = sb("ct_m", [P, 2 * NT * DIM], F16)
        yz = sb("yz", [P, CC, N], F32)
        zt = sb("zt", [P, 2 * 2 * 512], F16)
        kq = sb("kq", [P, 2, NT * HID], F16)
        ke = sb("ke", [P, 8, 512], F32)
        kmx = sb("kmx", [P, HC, NB], F32)
        nkm = sb("nkm", [P, HC], F32)
        ksum = sb("ksum", [P, HC], F32)
        krcp = sb("krcp", [P, HC], F32)
        qmx = sb("qmx", [P, 4, HEADS], BF16)
        qsum = sb("qsum", [P, 4, HEADS], F32)
        qrcp = sb("qrcp", [P, 4, HEADS], F32)
        st1 = sb("st1", [P, CC, NB, 6], F32)
        st2 = sb("st2", [P, CC, NB, 6], F32)
        mv1 = sb("mv1", [P, CC, 2], F32)
        mv2 = sb("mv2", [P, CC, 2], F32)
        ve1 = sb("ve1", [P, CC], F32)
        ve2 = sb("ve2", [P, CC], F32)
        rs1 = sb("rs1", [P, CC], F32)
        rs2 = sb("rs2", [P, CC], F32)
        lg = sb("lg", [P, CC, E_N], F32)
        top = sb("top", [P, CC, 8], F32)
        who = sb("who", [P, CC, 8], U32)
        whof = sb("whof", [P, CC, 8], F32)
        gd = sb("gd", [P, CC], F32)
        ge = sb("ge", [P, CC], F32)
        gs = sb("gs", [P, CC], F32)
        gw = sb("gw", [P, 2, CC], F32)
        gpick = sb("gpick", [P, CC, 2, E_N], F32)
        carrier = sb("carrier", [P, 1], F32)
        gfull = sb("gfull", [P, CC, E_N], F32)

        kt = kq[:, :, :].rearrange("p h (n d) -> p h n d", d=HID)
        qn = kq[:, :, :].rearrange("p h (j n) -> p h j n", n=N)
        kraw = ke[:, :, :].rearrange("p (s t) n -> p s (t n)", s=2)
        sq = ke[:, :, :].rearrange("p (b o) n -> p b o n", o=2)
        ct = ct_m[:, :].rearrange("p (h n c) -> p h n c", h=2, n=NT)
        kc = ct_m[:, 0:2048].rearrange("p (h c d) -> p h c d", h=2, c=CC)
        bd = ct_m[:, 2048:3072].rearrange("p (h d) -> p h d", h=2)
        mm = ct_m[:, 3072:5120].rearrange("p (h j o) -> p h j o", h=2, j=HC)
        bdf = ct_m[:, 5120:6144].bitcast(F32)
        mf = ct_m[:, 6144:8192].bitcast(F32).rearrange("p (j o) -> p j o", j=HC)
        z2t = zt[:, :].rearrange("p (s h n t) -> p s h n t", s=2, h=2, n=2)
        hwt = zt[:, :].rearrange("p (h j t) -> p h j t", h=2, j=HC)
        hw = yz[:, 0, 0:CC * HID].rearrange("p (t d) -> p t d", t=CC)

        raw_w = ct_m[:, :].bitcast(F32).rearrange("p (w n) -> p w n", w=4)
        raw_a = kq[:, :, :].rearrange("p h n -> p (h n)").bitcast(F32)
        raw_b = [yz[:, :, :].rearrange("p c n -> p (c n)"), xres[:, :, :].rearrange("p c n -> p (c n)")]

        ps = es.enter_context(nc.psum_tensor("ps", [P, 6, 512], F32))
        tp = es.enter_context(nc.psum_tensor("tp", [P, 2, 512], F32))

        w_in = [sem(f"w_in{i}") for i in range(4)]
        a_in, b_in, s_in = sem("a_in"), [sem("b_in0"), sem("b_in1")], sem("s_in")
        w_hi, w_lo = sem("w_hi"), sem("w_lo")
        consts, consts2, consts3 = sem("consts"), sem("consts2"), sem("consts3")
        ctx_in = [sem("ctx_in0"), sem("ctx_in1")]
        x_in = [sem("x_in0"), sem("x_in1")]
        res_in = sem("res_in")
        out_done = [sem("out_done0"), sem("out_done1")]
        ctx_hi, ctx_split = sem("ctx_hi"), sem("ctx_split")
        k_ready, k_copied = sem("k_ready"), sem("k_copied")
        k_max, k_exp = sem("k_max"), sem("k_exp")
        kmx_done = sem("kmx_done")
        ct_ready, ct_done = sem("ct_ready"), sem("ct_done")
        kt_ready, kt_hi, kt_done = sem("kt_ready"), sem("kt_hi"), sem("kt_done")
        st1_done, ln1_in, ln1_r = sem("st1_done"), sem("ln1_in"), sem("ln1_r")
        z1_f, z1_hi, z1_split = sem("z1_f"), sem("z1_hi"), sem("z1_split")
        kc_ready, kc_hi, kc_split = sem("kc_ready"), sem("kc_hi"), sem("kc_split")
        cx_ready, bd_f, bd_hi, bd_split = sem("cx_ready"), sem("bd_f"), sem("bd_hi"), sem("bd_split")
        kr_done = sem("kr_done")
        m_ready, m_read, m_hi, m_split = sem("m_ready"), sem("m_read"), sem("m_hi"), sem("m_split")
        q_ready, q_max, q_sub, q_exp = sem("q_ready"), sem("q_max"), sem("q_sub"), sem("q_exp")
        q_sum, q_rcp, q_nrm = sem("q_sum"), sem("q_rcp"), sem("q_nrm")
        qt_ready, qt_hi, qt_done = sem("qt_ready"), sem("qt_hi"), sem("qt_done")
        out_ready, out_y, out_used = sem("out_ready"), sem("out_y"), sem("out_used")
        sqs_ready, ss_ready, ss_used = sem("sqs_ready"), sem("ss_ready"), sem("ss_used")
        ln_done, rb_ready, t_done = sem("ln_done"), sem("rb_ready"), sem("t_done")
        x2_done = sem("x2_done")
        st2_done, ln2_in, ln2_r = sem("st2_done"), sem("ln2_in"), sem("ln2_r")
        z2_ready = sem("z2_ready")
        zt_ready, zt_hi, zt_done, zt_used = sem("zt_ready"), sem("zt_hi"), sem("zt_done"), sem("zt_used")
        ha_ready, gate_step, gate_exp = sem("ha_ready"), sem("gate_step"), sem("gate_exp")
        gate_read, hw_done = sem("gate_read"), sem("hw_done")
        ht_ready, ht_hi, ht_done = sem("ht_ready"), sem("ht_hi"), sem("ht_done")
        y_ready, fin_done = sem("y_ready"), sem("fin_done")
        G_STEPS = 14

        block = es.enter_context(nc.Block())

        def turns(eng, body):
            body(Turn(None, 0), None, True)
            with eng.Fori(0, B - 2) as i:
                body(Turn(i, 1), Turn(i, 0), True)
            body(Turn(None, B - 1), Turn(None, B - 2), False)
            body(None, Turn(None, B - 1), False)

        WEIGHTS = [(raw_w[:, i, :], w_in[i], w) for i, w in enumerate((
            wk[:, :, :, :].rearrange("p h c n -> p h (c n)"), wq[:, :, :, :].rearrange("p h c n -> p h (c n)"),
            wv[:, :, :, :].rearrange("p h c n -> p h (c n)"), wo[:, :, :, :].rearrange("p h c n -> p h (c n)")))]
        wa_f = wa[:, :, :, :].rearrange("p h c n -> p h (c n)")
        wb_f = wb[:, :, :, :].rearrange("p h c n -> p h (c n)")
        WEIGHTS.append((wg_raw[:, :, :].rearrange("p c n -> p (c n)"), s_in, wg[:, :, :, :].rearrange("p h c n -> p h (c n)")))
        for i in range(4):
            WEIGHTS.append((raw_a[:, i * 2048:(i + 1) * 2048], a_in, wa_f[:, :, i * 2048:(i + 1) * 2048]))
        for i in range(4):
            WEIGHTS.append((raw_b[i // 2][:, (i % 2) * 2048:(i % 2 + 1) * 2048], b_in[i // 2],
                            wb_f[:, :, i * 2048:(i + 1) * 2048]))
        W_PARTS = len(WEIGHTS)

        @block.sync
        def _(sp):
            def load_ctx(a):
                for c in range(CC):
                    sp.dma_start(stage[:, c, :], c_v[a.index, :, c, :]).then_inc(ctx_in[c], 16)

            def load_x(a):
                for c in range(CC):
                    sp.wait_ge(ctx_split, a.at(2, c + 1))
                    sp.dma_start(stage[:, c, :], x_v[a.index, :, c, :]).then_inc(x_in[c], 16)

            load_ctx(Turn(None, 0))
            for i, w in enumerate((wkT, wqT, wvT, woT)):
                sp.dma_start(raw_w[:, i, :], w).then_inc(w_in[i], 16)
            for dst, src in ((wg_raw[:, :, :], gateT), (bo_c[:, :], bo), (g_c[:, :], g)):
                sp.dma_start(dst, src).then_inc(s_in, 16)
            sp.dma_start(raw_a, aT).then_inc(a_in, 16)
            for i in range(2):
                sp.dma_start(raw_b[i], bT[:, i * 4096:(i + 1) * 4096]).then_inc(b_in[i], 16)
            load_x(Turn(None, 0))

            def body(a, f, more):
                if more:
                    for c in range(CC):
                        sp.wait_ge(z1_split, a.at(2, c + 1))
                        sp.dma_start(stage[:, c, :], c_v[a.next.index, :, c, :]).then_inc(ctx_in[c], 16)
                if f:
                    for c in range(CC):
                        sp.wait_ge(fin_done, f.at(8, 4 * c + 4))
                        sp.dma_start(o_v[f.index, :, c, :], xres[:, c, :]).then_inc(out_done[c], 16)
                    for c in range(CC):
                        sp.wait_ge(out_done[c], f.at(16, 16))
                else:
                    sp.wait_ge(w_lo, W_PARTS)
                if a:
                    sp.dma_start(xres[:, :, :], x_v[a.index]).then_inc(res_in, 16)
                if more:
                    load_x(a.next)

            turns(sp, body)

        @block.gpsimd
        def _(pool):
            nc.gpsimd.memset(ident[:, :], 0.0).then_inc(consts, 1)
            nc.gpsimd.memset(ones[:, :], 1.0).then_inc(consts, 1)
            nc.gpsimd.memset(minus_half[:, :], -0.5).then_inc(consts, 1)
            for e in range(E_N):
                nc.gpsimd.memset(experts[:, e:e + 1], float(e)).then_inc(consts, 1)
            pool.wait_ge(consts, 11)
            nc.gpsimd.affine_select(out=ident[:, :], in_=ident[:, :], compare_op=ALU.not_equal, fill=1.0,
                                    base=0, pattern=[[-1, P]], channel_multiplier=1).then_inc(consts, 1)

            def body(a, f, more):
                if f:
                    add_x(f, 2)
                    add_x(f, 3)
                    pool.wait_ge(ln2_in, f.at(3, 3))
                    nc.gpsimd.tensor_tensor(rs2[:, :], ve2[:, :], minus_half[:, :], ALU.pow).then_inc(ln2_r, 1)
                if a:
                    pool.wait_ge(ln1_in, a.at(3, 3))
                    nc.gpsimd.tensor_tensor(rs1[:, :], ve1[:, :], minus_half[:, :], ALU.pow).then_inc(ln1_r, 1)
                    for i in range(NT):
                        pool.wait_ge(q_rcp, a.at(16, i + 1))
                        e = ke[:, i % 8, :].rearrange("p (h d) -> p h d", h=HEADS)
                        r = qrcp[:, i % 4, :].unsqueeze(2).to_broadcast([P, HEADS, DH])
                        nc.gpsimd.tensor_tensor(e, e, r, ALU.mult).then_inc(q_nrm, 1)
                    pool.wait_ge(res_in, a.at(16, 16))
                    add_x(a, 0)
                    add_x(a, 1)

            def add_x(t, nb):
                pool.wait_ge(t_done, t.at(8, 2 * nb + 2))
                cols = slice(nb * 512, nb * 512 + 512)
                nc.gpsimd.tensor_tensor(xres[:, :, cols], xres[:, :, cols], yz[:, :, cols],
                                        ALU.add).then_inc(x2_done, 1)

            turns(pool, body)

        @block.scalar
        def _(act):
            def split_ctx(a):
                for c in range(CC):
                    act.wait_ge(ctx_in[c], a.at(16, 16))
                    nc.scalar.activation(opnd[:, HI, c, :], stage[:, c, :], ACT.Copy, scale=S_C).then_inc(ctx_hi, 1)

            split_ctx(Turn(None, 0))
            for i, (raw, landed, parts) in enumerate(WEIGHTS):
                act.wait_ge(landed, 48 if landed is s_in else 16)
                nc.scalar.activation(parts[:, HI, :], raw, ACT.Copy, scale=S_W).then_inc(w_hi, 1)
            act.wait_ge(w_lo, W_PARTS)

            def exp_k(a, j):
                act.wait_ge(k_max, a.at(4, j + 1))
                nc.scalar.activation(kraw[:, j % 2, :], kraw[:, j % 2, :], ACT.Exp, bias=nkm[:, j:j + 1],
                                     accum_out=ksum[:, j:j + 1]).then_inc(k_exp, 1)

            def kt_high(a, kg):
                act.wait_ge(kt_ready, a.at(16, kg + 1))
                j, t = kg // 4, kg % 4
                src = tp[:, kt_bank(kg), :].rearrange("p (n d) -> p n d", n=4)
                nc.scalar.activation(kt[:, HI, 4 * t:4 * t + 4, j * P:(j + 1) * P], src, ACT.Copy,
                                     scale=S_K).then_inc(kt_hi, 1)

            def row_scale(t, nb):
                act.wait_ge(ss_used, t.at(4, nb + 1))
                nc.scalar.activation(sq[:, nb, 1, :], sq[:, nb, 1, :], ACT.Ln, scale=S_N).then_inc(ln_done, 1)
                act.wait_ge(ln_done, t.at(4, nb + 1))
                nc.scalar.activation(sq[:, nb, 1, :], sq[:, nb, 1, :], ACT.Exp, scale=-0.5).then_inc(rb_ready, 1)

            def body(a, f, more):
                for i in range(KTILES if a else 0):
                    if f and i % 4 == 0 and i < 8:
                        act.wait_ge(t_done, f.at(8, 4 + i))
                    act.wait_ge(k_ready, a.at(16, i + 1))
                    nc.scalar.activation(ke[:, i % 8, :], ps[:, RING[i % 4], :], ACT.Copy,
                                         scale=1.0 / (S_C * S_W)).then_inc(k_copied, 1)
                    if f and i == 1:
                        row_scale(f, 3)
                    if i % 4 == 1 and i > 4:
                        exp_k(a, i // 4 - 1)
                    if i % 2:
                        act.wait_ge(ct_ready, a.at(8, i // 2 + 1))
                        src = tp[:, 0, :].bitcast(F16).rearrange("p (h n c) -> p h n c", h=2, n=2)
                        nc.scalar.activation(ct[:, :, i - 1:i + 1, :], src, ACT.Copy).then_inc(ct_done, 1)
                    if i >= KT_LAG:
                        kt_high(a, i - KT_LAG)
                if f and not a:
                    row_scale(f, 3)
                if a:
                    exp_k(a, 3)
                for gr in range(GROUPS):
                    if a and 9 + gr < KTILES:
                        kt_high(a, 9 + gr)
                    if f:
                        act.wait_ge(zt_ready, f.at(8, gr + 1))
                        if gr >= 2:
                            act.wait_ge(zt_used, f.at(GROUPS - 1, gr - 1))
                        nc.scalar.activation(z2t[:, gr % 2, HI, :, :], tp[:, 1, :].rearrange("p (n t) -> p n t", n=2),
                                             ACT.Copy, scale=S_Z).then_inc(zt_hi, 1)
                if a:
                    act.wait_ge(ct_ready, a.at(8, 8))
                    for c in range(CC):
                        act.wait_ge(z1_f, a.at(2, c + 1))
                        nc.scalar.activation(opnd[:, HI, c, :], stage[:, c, :], ACT.Copy, scale=S_Z).then_inc(z1_hi, 1)
                if f:
                    act.wait_ge(gate_step, f.at(G_STEPS, G_DIFF))
                    nc.scalar.activation(ge[:, :], gd[:, :], ACT.Exp).then_inc(gate_exp, 1)
                if a:
                    for c in range(CC):
                        act.wait_ge(kc_ready, a.at(2, c + 1))
                        nc.scalar.activation(kc[:, HI, c, :], ps[:, KC_BANK[c], :], ACT.Copy,
                                             scale=1.0 / (S_K * S_C)).then_inc(kc_hi, 1)
                for s in range(1, NT + Q_LAG if a else 0):
                    if s <= NT:
                        act.wait_ge(q_sub, a.at(16, s))
                        nc.scalar.activation(ke[:, (s - 1) % 8, :], ps[:, RING[(s - 1) % 4], :], ACT.Exp,
                                             scale=1.0 / (S_Z * S_W)).then_inc(q_exp, 1)
                    if s == BD_AT:
                        act.wait_ge(bd_f, a.at(1, 1))
                        nc.scalar.activation(bd[:, HI, :], bdf, ACT.Copy).then_inc(bd_hi, 1)
                    if s == M_AT:
                        act.wait_ge(m_read, a.at(4, 4))
                        nc.scalar.activation(mm[:, HI, :, :], mf, ACT.Copy).then_inc(m_hi, 1)
                    if s >= Q_LAG:
                        i = s - Q_LAG
                        act.wait_ge(qt_ready, a.at(16, i + 1))
                        nc.scalar.activation(qn[:, HI, :, i * P:(i + 1) * P],
                                             tp[:, i % 2, :].rearrange("p (j n) -> p j n", j=HC),
                                             ACT.Copy, scale=S_Q).then_inc(qt_hi, 1)
                if f:
                    for t in range(CC):
                        act.wait_ge(ht_ready, f.at(2, t + 1))
                        nc.scalar.activation(hwt[:, HI, :, t * P:(t + 1) * P],
                                             tp[:, t, :].rearrange("p (j n) -> p j n", j=HC), ACT.Copy).then_inc(ht_hi, 1)
                if more:
                    act.wait_ge(q_ready, a.at(16, 16))
                    split_ctx(a.next)
                for nb in range(NB if a else 0):
                    for o in range(CC):
                        i = nb * CC + o
                        act.wait_ge(out_ready, a.at(8, i + 1))
                        tile = ps[:, RING[i % 4], :]
                        nc.scalar.activation(yz[:, o, nb * 512:nb * 512 + 512], tile, ACT.Identity,
                                             bias=bo_c[:, o:o + 1], scale=DH**-0.5 / (S_M * S_Q)).then_inc(out_y, 1)
                        nc.scalar.activation(sq[:, nb, o, :], tile, ACT.Square,
                                             bias=bo_c[:, o:o + 1], scale=DH**-0.5 / (S_M * S_Q)).then_inc(out_used, 1)
                    if nb:
                        row_scale(a, nb - 1)

            G_DIFF = 6
            turns(act, body)

        @block.vector
        def _(dve):
            def low(out_, raw, scale, high):
                return nc.vector.scalar_tensor_tensor(out=out_, in0=raw, scalar=scale, in1=high,
                                                      op0=ALU.mult, op1=ALU.subtract)

            def split_ctx(a):
                for c in range(CC):
                    dve.wait_ge(ctx_hi, a.at(2, c + 1))
                    low(opnd[:, LO, c, :], stage[:, c, :], S_C, opnd[:, HI, c, :]).then_inc(ctx_split, 1)

            split_ctx(Turn(None, 0))
            for i, (raw, landed, parts) in enumerate(WEIGHTS):
                dve.wait_ge(w_hi, i + 1)
                low(parts[:, LO, :], raw, S_W, parts[:, HI, :]).then_inc(w_lo, 1)
            nc.vector.memset(pairmask[:, :], 0.0).then_inc(consts3, 1)
            dve.wait_ge(consts3, 1)
            nc.vector.memset(pairmask[0:DH, 0:DH], 1.0).then_inc(consts3, 1)
            nc.vector.memset(pairmask[DH:P, DH:P], 1.0).then_inc(consts3, 1)
            dve.wait_ge(consts, 12)
            nc.vector.tensor_copy(ident16[:, :], ident[:, :]).then_inc(consts2, 1)
            nc.vector.tensor_scalar(minus1[:, :], ident[:, :], -1.0, None, ALU.mult).then_inc(consts2, 1)
            nc.vector.tensor_scalar(g_c[:, :], g_c[:, :], DIM**0.5 * S_N**0.5, None, ALU.mult).then_inc(consts2, 1)
            dve.wait_ge(consts2, 3)
            dve.wait_ge(consts3, 3)

            def carry():
                nc.vector.memset(carrier[:, :], 0.0)

            def max_k(a, i):
                dve.wait_ge(k_copied, a.at(16, i + 1))
                nc.vector.reduce_max(kmx[:, i // 4, i % 4:i % 4 + 1], ke[:, i % 8, :], X).then_inc(kmx_done, 1)
                if i % 4 == 3:
                    dve.wait_ge(kmx_done, a.at(16, i + 1))
                    nc.vector.tensor_reduce(nkm[:, i // 4:i // 4 + 1], kmx[:, i // 4, :], X, ALU.max,
                                            negate=True).then_inc(k_max, 1)

            def kt_low(a, kg):
                dve.wait_ge(kt_hi, a.at(16, kg + 1))
                j, t = kg // 4, kg % 4
                src = tp[:, kt_bank(kg), :].rearrange("p (n d) -> p n d", n=4)
                where = (slice(4 * t, 4 * t + 4), slice(j * P, (j + 1) * P))
                low(kt[:, LO, where[0], where[1]], src, S_K, kt[:, HI, where[0], where[1]]).then_inc(kt_done, 1)

            def floor_norm(t, nb):
                dve.wait_ge(ss_ready, t.at(4, nb + 1))
                nc.vector.tensor_scalar(sq[:, nb, 1, :], ps[:, PAIR[nb % 2], :], NORM_FLOOR**2, None,
                                        ALU.max).then_inc(ss_used, 1)

            def scale_y(t, nb):
                dve.wait_ge(rb_ready, t.at(4, nb + 1))
                for o in range(CC):
                    y = yz[:, o, nb * 512:nb * 512 + 512]
                    nc.vector.scalar_tensor_tensor(out=y, in0=y, scalar=g_c[:, o:o + 1], in1=sq[:, nb, 1, :],
                                                   op0=ALU.mult, op1=ALU.mult).then_inc(t_done, 1)

            def stats2(f, nb):
                dve.wait_ge(x2_done, f.at(4, nb + 1))
                for o in range(CC):
                    nc.vector.bn_stats(st2[:, o, nb, :], xres[:, o, nb * 512:nb * 512 + 512]).then_inc(st2_done, 1)

            def mean_var(t, st_done, st, mv, ve, ln_in):
                dve.wait_ge(st_done, t.at(8, 8))
                carry()
                for o in range(CC):
                    nc.vector.bn_aggr(mv[:, o, :], st[:, o, :, :].rearrange("p b s -> p (b s)")).then_inc(ln_in, 1)
                dve.wait_ge(ln_in, t.at(3, 2))
                nc.vector.tensor_scalar(ve[:, :], mv[:, :, 1], LN_EPS, None, ALU.add).then_inc(ln_in, 1)

            def z2_rows(f, o):
                if o == 0:
                    dve.wait_ge(ln2_r, f.at(1, 1))
                nc.vector.tensor_scalar(yz[:, o, :], xres[:, o, :], mv2[:, o, 0:1], rs2[:, o:o + 1],
                                        ALU.subtract, ALU.mult).then_inc(z2_ready, 1)

            def gate(f):
                n = [0]

                def step(ins, wait=True):
                    n[0] += 1
                    ins.then_inc(gate_step, 1)
                    if wait:
                        dve.wait_ge(gate_step, f.at(G_STEPS, n[0]))

                dve.wait_ge(ha_ready, f.at(1, 1))
                nc.vector.tensor_scalar(lg[:, :, :], ps[:, GATE_BANK, 0:CC * E_N].rearrange("p (t e) -> p t e", t=CC),
                                        1.0 / (S_Z * S_W), None, ALU.mult).then_inc(gate_read, 1)
                dve.wait_ge(gate_read, f.at(1, 1))
                carry()
                step(nc.vector.max(top[:, 0, :], lg[:, 0, :]), False)
                step(nc.vector.max(top[:, 1, :], lg[:, 1, :]), False)
                dve.wait_ge(gate_step, f.at(G_STEPS, 2))
                carry()
                step(nc.vector.max_index(who[:, 0, :], top[:, 0, :], lg[:, 0, :]), False)
                step(nc.vector.max_index(who[:, 1, :], top[:, 1, :], lg[:, 1, :]))
                step(nc.vector.tensor_copy(whof[:, :, :], who[:, :, :]), False)
                step(nc.vector.tensor_tensor(gd[:, :], top[:, :, 1], top[:, :, 0], ALU.subtract))
                dve.wait_ge(gate_exp, f.at(1, 1))
                step(nc.vector.tensor_scalar(gs[:, :], ge[:, :], 1.0, None, ALU.add))
                step(nc.vector.reciprocal(gw[:, 0, :], gs[:, :]))
                step(nc.vector.tensor_tensor(gw[:, 1, :], ge[:, :], gw[:, 0, :], ALU.mult))
                for t in range(CC):
                    for r in range(2):
                        step(nc.vector.tensor_scalar(gpick[:, t, r, :], experts[:, :], whof[:, t, r:r + 1],
                                                     gw[:, r, t:t + 1], ALU.is_equal, ALU.mult), t + r == 2)
                step(nc.vector.tensor_tensor(gfull[:, :, :], gpick[:, :, 0, :], gpick[:, :, 1, :], ALU.add))
                assert n[0] == G_STEPS
                for t in range(CC):
                    nc.vector.scalar_tensor_tensor(
                        out=hw[:, t, :].rearrange("p (e r) -> p e r", e=E_N),
                        in0=ps[:, PAIR[t], :].rearrange("p (e r) -> p e r", e=E_N), scalar=S_H / (S_Z * S_W),
                        in1=gfull[:, t, :].unsqueeze(2).to_broadcast([P, E_N, DH]),
                        op0=ALU.mult, op1=ALU.mult).then_inc(hw_done, 1)

            def body(a, f, more):
                tail = {}
                if f:
                    tail = {0: [(scale_y, 2)], 1: [(floor_norm, 3), (stats2, 0)], 2: [(scale_y, 3)],
                            3: [(stats2, 1)], 4: [(stats2, 2)], 6: [(stats2, 3)]}
                for i in range(KTILES):
                    if a:
                        max_k(a, i)
                        if i >= KT_LAG:
                            kt_low(a, i - KT_LAG)
                    for what, nb in tail.get(i, []):
                        what(f, nb)
                    if f and i == 7:
                        mean_var(f, st2_done, st2, mv2, ve2, ln2_in)
                    if f and i in (9, 10):
                        z2_rows(f, i - 9)
                for gr in range(GROUPS):
                    if a and 9 + gr < KTILES:
                        kt_low(a, 9 + gr)
                    if f:
                        dve.wait_ge(zt_hi, f.at(8, gr + 1))
                        low(z2t[:, gr % 2, LO, :, :], tp[:, 1, :].rearrange("p (n t) -> p n t", n=2), S_Z,
                            z2t[:, gr % 2, HI, :, :]).then_inc(zt_done, 1)
                    if a:
                        o, nb = gr // NB, gr % NB
                        if nb == 0:
                            dve.wait_ge(x_in[o], a.at(16, 16))
                        nc.vector.bn_stats(st1[:, o, nb, :], stage[:, o, nb * 512:nb * 512 + 512]).then_inc(st1_done, 1)
                if a:
                    mean_var(a, st1_done, st1, mv1, ve1, ln1_in)
                    dve.wait_ge(ln1_r, a.at(1, 1))
                    for o in range(CC):
                        nc.vector.tensor_scalar(stage[:, o, :], stage[:, o, :], mv1[:, o, 0:1], rs1[:, o:o + 1],
                                                ALU.subtract, ALU.mult).then_inc(z1_f, 1)
                    for o in range(CC):
                        dve.wait_ge(z1_hi, a.at(2, o + 1))
                        low(opnd[:, LO, o, :], stage[:, o, :], S_Z, opnd[:, HI, o, :]).then_inc(z1_split, 1)
                    dve.wait_ge(k_exp, a.at(4, 4))
                    nc.vector.reciprocal(krcp[:, :], ksum[:, :]).then_inc(kr_done, 1)
                if f:
                    gate(f)
                if a:
                    for c in range(CC):
                        dve.wait_ge(kc_hi, a.at(2, c + 1))
                        low(kc[:, LO, c, :], ps[:, KC_BANK[c], :], 1.0 / (S_K * S_C), kc[:, HI, c, :]).then_inc(kc_split, 1)
                for s in range(NT + Q_LAG + 1 if a else 0):
                    if s >= Q_LAG + 1:
                        i = s - Q_LAG - 1
                        dve.wait_ge(qt_hi, a.at(16, i + 1))
                        cols = slice(i * P, (i + 1) * P)
                        low(qn[:, LO, :, cols], tp[:, i % 2, :].rearrange("p (j n) -> p j n", j=HC), S_Q,
                            qn[:, HI, :, cols]).then_inc(qt_done, 1)
                    if s < NT:
                        dve.wait_ge(q_ready, a.at(16, s + 1))
                        nc.vector.reduce_max(qmx[:, s % 4, :],
                                             ps[:, RING[s % 4], :].rearrange("p (h d) -> p h d", h=HEADS),
                                             X).then_inc(q_max, 1)
                    if 1 <= s <= NT:
                        i = s - 1
                        dve.wait_ge(q_exp, a.at(16, i + 1))
                        if i >= 4:
                            dve.wait_ge(q_nrm, a.at(16, i - 3))
                        nc.vector.reduce_sum(qsum[:, i % 4, :], ke[:, i % 8, :].rearrange("p (h d) -> p h d", h=HEADS),
                                             X).then_inc(q_sum, 1)
                        dve.wait_ge(q_sum, a.at(16, i + 1))
                        nc.vector.reciprocal(qrcp[:, i % 4, :], qsum[:, i % 4, :]).then_inc(q_rcp, 1)
                    if s == BD_AT - 1:
                        dve.wait_ge(cx_ready, a.at(1, 1))
                        nc.vector.scalar_tensor_tensor(
                            out=bdf.rearrange("p (j d) -> p j d", j=HC),
                            in0=ps[:, PAIR[0], :].rearrange("p (j d) -> p j d", j=HC), scalar=1.0 / S_W,
                            in1=pairmask[:, :].unsqueeze(1).to_broadcast([P, HC, P]),
                            op0=ALU.mult, op1=ALU.mult).then_inc(bd_f, 1)
                    if s == BD_AT:
                        dve.wait_ge(bd_hi, a.at(1, 1))
                        nc.vector.tensor_tensor(bd[:, LO, :], bdf, bd[:, HI, :], ALU.subtract).then_inc(bd_split, 1)
                    if s == M_AT - 1:
                        dve.wait_ge(kr_done, a.at(1, 1))
                        for j in range(HC):
                            if j % 2 == 0:
                                dve.wait_ge(m_ready, a.at(2, j // 2 + 1))
                            nc.vector.tensor_scalar(mf[:, j, :], ps[:, PAIR[1 - j // 2], (j % 2) * DIM:(j % 2 + 1) * DIM],
                                                    krcp[:, j:j + 1], S_M / S_W, ALU.mult, ALU.mult).then_inc(m_read, 1)
                    if s == M_AT:
                        dve.wait_ge(m_hi, a.at(1, 1))
                        nc.vector.tensor_tensor(mm[:, LO, :, :], mf, mm[:, HI, :, :], ALU.subtract).then_inc(m_split, 1)
                if f:
                    for t in range(CC):
                        dve.wait_ge(ht_hi, f.at(2, t + 1))
                        low(hwt[:, LO, :, t * P:(t + 1) * P], tp[:, t, :].rearrange("p (j n) -> p j n", j=HC), 1.0,
                            hwt[:, HI, :, t * P:(t + 1) * P]).then_inc(ht_done, 1)
                    for u in range(8):
                        t, nb = u // NB, u % NB
                        dve.wait_ge(y_ready, f.at(8, u + 1))
                        acc = xres[:, t, nb * 512:nb * 512 + 512]
                        nc.vector.scalar_tensor_tensor(out=acc, in0=ps[:, PAIR[u % 2], :], scalar=1.0 / (S_H * S_W),
                                                       in1=acc, op0=ALU.mult, op1=ALU.add).then_inc(fin_done, 1)
                        if u == 3 and more:
                            split_ctx(a.next)
                elif more:
                    split_ctx(a.next)
                for nb in range(NB if a else 0):
                    dve.wait_ge(out_used, a.at(8, 2 * nb + 2))
                    nc.vector.tensor_tensor(sq[:, nb, 0, :], sq[:, nb, 0, :], sq[:, nb, 1, :], ALU.add).then_inc(sqs_ready, 1)
                    if nb >= 1:
                        floor_norm(a, nb - 1)
                    if nb >= 2:
                        scale_y(a, nb - 2)

            turns(dve, body)

        @block.tensor
        def _(pe):
            def mac3(acc, l_hi, l_lo, r_hi, r_lo, first, last):
                nc.tensor.matmul(acc, l_hi, r_hi, start=first, stop=False)
                nc.tensor.matmul(acc, l_hi, r_lo, start=False, stop=False)
                return nc.tensor.matmul(acc, l_lo, r_hi, start=False, stop=last)

            pe.wait_ge(consts2, 3)

            def norms(t, nb):
                pe.wait_ge(sqs_ready, t.at(4, nb + 1))
                nc.tensor.matmul(ps[:, PAIR[nb % 2], :], ones[:, :], sq[:, nb, 0, :],
                                 start=True, stop=True).then_inc(ss_ready, 1)

            def kt_blocks(a, kg):
                j, t = kg // 4, kg % 4
                if t == 0:
                    pe.wait_ge(k_exp, a.at(4, j + 1))
                for q in range(4):
                    n = 4 * t + q
                    last = nc.tensor.transpose(tp[:, kt_bank(kg), q * P:(q + 1) * P],
                                               kraw[:, j % 2, n * P:(n + 1) * P], ident[:, :])
                last.then_inc(kt_ready, 1)

            def body(a, f, more):
                for i in range(KTILES if a else 0):
                    j, nb = i // NB, i % NB
                    if i == 0:
                        pe.wait_ge(ctx_split, a.at(2, 2))
                    if i >= 4:
                        pe.wait_ge(k_copied, a.at(16, i - 3))
                    elif f:
                        pe.wait_ge(out_used, f.at(8, 5 + i))
                    acc = ps[:, RING[i % 4], :]
                    for c in range(CC):
                        last = mac3(acc, wk[:, HI, c, j * P:(j + 1) * P], wk[:, LO, c, j * P:(j + 1) * P],
                                    opnd[:, HI, c, nb * 512:nb * 512 + 512], opnd[:, LO, c, nb * 512:nb * 512 + 512],
                                    c == 0, c == CC - 1)
                    last.then_inc(k_ready, 1)
                    if f and i == 1:
                        pe.wait_ge(ss_used, f.at(4, 2))
                        norms(f, 3)
                    if i % 2:
                        m = i // 2
                        if i - 1 >= KT_LAG:
                            pe.wait_ge(kt_done, a.at(16, i - KT_LAG))
                        elif m:
                            pe.wait_ge(ct_done, a.at(8, m))
                        dst = tp[:, 0, :].bitcast(F16).rearrange("p (h n c) -> p h n c", h=2, n=2)
                        for h in range(2):
                            for q in range(2):
                                for c in range(CC):
                                    n = 2 * m + q
                                    last = nc.tensor.transpose(dst[:, h, q, c * P:(c + 1) * P],
                                                               opnd[:, h, c, n * P:(n + 1) * P], ident16[:, :])
                        last.then_inc(ct_ready, 1)
                    if i >= KT_LAG:
                        kg = i - KT_LAG
                        if i % 2 == 0:
                            pe.wait_ge(ct_done, a.at(8, i // 2))
                        elif kg >= 2:
                            pe.wait_ge(kt_done, a.at(16, kg - 1))
                        kt_blocks(a, kg)
                if f and not a:
                    pe.wait_ge(ss_used, f.at(4, 2))
                    norms(f, 3)

                def z2_blocks(gr):
                    for q in range(2):
                        for t in range(CC):
                            n = 2 * gr + q
                            last = nc.tensor.transpose(tp[:, 1, (q * CC + t) * P:(q * CC + t + 1) * P],
                                                       yz[:, t, n * P:(n + 1) * P], ident[:, :])
                    last.then_inc(zt_ready, 1)

                if f:
                    if a:
                        pe.wait_ge(kt_done, a.at(16, 9))
                    pe.wait_ge(z2_ready, f.at(2, 2))
                    z2_blocks(0)
                for gr in range(GROUPS):
                    if a and 9 + gr < KTILES:
                        if gr == 0:
                            pe.wait_ge(ct_done, a.at(8, 8))
                        else:
                            pe.wait_ge(kt_done, a.at(16, 9 + gr))
                        kt_blocks(a, 9 + gr)
                    if not f:
                        continue
                    pe.wait_ge(zt_done, f.at(8, gr + 1))
                    if gr + 1 < GROUPS:
                        z2_blocks(gr + 1)
                    if gr == 0:
                        if a:
                            pe.wait_ge(k_copied, a.at(16, 13))
                        else:
                            pe.wait_ge(out_used, f.at(8, 5))
                    for q in range(2):
                        n = 2 * gr + q
                        for t in range(CC):
                            if gr == 0 and q == 0:
                                pe.wait_ge(ss_used, f.at(4, 3 + t))
                            z_hi = z2t[:, gr % 2, HI, q, t * P:(t + 1) * P]
                            z_lo = z2t[:, gr % 2, LO, q, t * P:(t + 1) * P]
                            ranks = ps[:, PAIR[t], :]
                            logits = ps[:, GATE_BANK, t * E_N:(t + 1) * E_N]
                            first, final = n == 0, n == NT - 1
                            nc.tensor.matmul(ranks, z_hi, wa[:, HI, n, :], start=first, stop=False)
                            nc.tensor.matmul(ranks, z_hi, wa[:, LO, n, :], start=False, stop=False)
                            nc.tensor.matmul(logits, z_hi, wg[:, HI, n, :], start=first and t == 0, stop=False,
                                             skip_group_check=True)
                            nc.tensor.matmul(logits, z_hi, wg[:, LO, n, :], start=False, stop=False,
                                             skip_group_check=True)
                            nc.tensor.matmul(ranks, z_lo, wa[:, HI, n, :], start=False, stop=final)
                            nc.tensor.matmul(logits, z_lo, wg[:, HI, n, :], start=False, stop=False,
                                             skip_group_check=True)
                            last = nc.tensor.matmul(logits, z_lo, wg[:, LO, n, :], start=False, stop=final,
                                                    skip_group_check=True)
                    last.then_inc(ha_ready if gr == GROUPS - 1 else zt_used, 1)

                if a:
                    pe.wait_ge(k_copied, a.at(16, 16))
                    pe.wait_ge(ct_done, a.at(8, 8))
                    pe.wait_ge(kt_done, a.at(16, 16))
                    for n in range(NT):
                        for c in range(CC):
                            last = mac3(ps[:, KC_BANK[c], :], ct[:, HI, n, c * P:(c + 1) * P],
                                        ct[:, LO, n, c * P:(c + 1) * P], kt[:, HI, n, :], kt[:, LO, n, :],
                                        n == 0, n == NT - 1)
                            if n == NT - 1:
                                last.then_inc(kc_ready, 1)

                for s in range(NT + Q_LAG if a else 0):
                    if s < NT:
                        if s == 0:
                            pe.wait_ge(z1_split, a.at(2, 2))
                            if f:
                                pe.wait_ge(gate_read, f.at(1, 1))
                        elif s in (2, 3):
                            pe.wait_ge(kc_split, a.at(2, s - 1))
                        elif s >= 4:
                            pe.wait_ge(q_exp, a.at(16, s - 3))
                        for c in range(CC):
                            last = mac3(ps[:, RING[s % 4], :], opnd[:, HI, c, s * P:(s + 1) * P],
                                        opnd[:, LO, c, s * P:(s + 1) * P], wq[:, HI, c, :], wq[:, LO, c, :],
                                        c == 0, c == CC - 1)
                        last.then_inc(q_ready, 1)
                    if 1 <= s <= NT:
                        i = s - 1
                        pe.wait_ge(q_max, a.at(16, i + 1))
                        nc.tensor.matmul(ps[:, RING[i % 4], :].rearrange("p (h d) -> p h d", h=HEADS), minus1[:, :],
                                         qmx[:, i % 4, :].unsqueeze(2).to_broadcast([P, HEADS, DH]),
                                         start=False, stop=True, skip_group_check=True).then_inc(q_sub, 1)
                    if s == CX_AT:
                        if f:
                            pe.wait_ge(hw_done, f.at(2, 1))
                        for j in range(HC):
                            two = slice(j * P, (j + 1) * P)
                            for c in range(CC):
                                last = mac3(ps[:, PAIR[0], two], wv[:, HI, c, two], wv[:, LO, c, two],
                                            kc[:, HI, c, two], kc[:, LO, c, two], c == 0, c == CC - 1)
                        last.then_inc(cx_ready, 1)
                    if s == MM_AT:
                        if f:
                            pe.wait_ge(hw_done, f.at(2, 2))
                        pe.wait_ge(bd_split, a.at(1, 1))
                        for j in range(HC):
                            two = slice(j * P, (j + 1) * P)
                            last = mac3(ps[:, PAIR[1 - j // 2], (j % 2) * DIM:(j % 2 + 1) * DIM],
                                        bd[:, HI, two], bd[:, LO, two], wo[:, HI, j, :], wo[:, LO, j, :], True, True)
                            if j % 2:
                                last.then_inc(m_ready, 1)
                    if s >= Q_LAG:
                        i = s - Q_LAG
                        pe.wait_ge(q_nrm, a.at(16, i + 1))
                        if i >= 2:
                            pe.wait_ge(qt_done, a.at(16, i - 1))
                        for j in range(HC):
                            last = nc.tensor.transpose(tp[:, i % 2, j * P:(j + 1) * P],
                                                       ke[:, i % 8, j * P:(j + 1) * P], ident[:, :])
                        last.then_inc(qt_ready, 1)

                if f:
                    for t in range(CC):
                        pe.wait_ge(hw_done, f.at(2, t + 1))
                        if a:
                            pe.wait_ge(qt_done, a.at(16, 15 + t))
                        for j in range(HC):
                            last = nc.tensor.transpose(tp[:, t, j * P:(j + 1) * P], hw[:, t, j * P:(j + 1) * P],
                                                       ident[:, :])
                        last.then_inc(ht_ready, 1)
                    for u in range(8):
                        t, nb = u // NB, u % NB
                        if u == 0 and a:
                            pe.wait_ge(m_read, a.at(4, 4))
                        if nb == 0:
                            pe.wait_ge(ht_done, f.at(2, t + 1))
                        if u >= 2:
                            pe.wait_ge(fin_done, f.at(8, u - 1))
                        for j in range(HC):
                            last = mac3(ps[:, PAIR[u % 2], :], hwt[:, HI, j, t * P:(t + 1) * P],
                                        hwt[:, LO, j, t * P:(t + 1) * P], wb[:, HI, j, nb * 512:nb * 512 + 512],
                                        wb[:, LO, j, nb * 512:nb * 512 + 512], j == 0, j == HC - 1)
                        last.then_inc(y_ready, 1)

                for i in range(8 if a else 0):
                    nb, o = i // CC, i % CC
                    if i == 0:
                        pe.wait_ge(qt_done, a.at(16, 16))
                        pe.wait_ge(m_split, a.at(1, 1))
                    if i < 4:
                        pe.wait_ge(q_exp, a.at(16, 13 + i))
                    else:
                        pe.wait_ge(out_used, a.at(8, i - 3))
                    for j in range(HC):
                        last = mac3(ps[:, RING[i % 4], :], mm[:, HI, j, o * P:(o + 1) * P], mm[:, LO, j, o * P:(o + 1) * P],
                                    qn[:, HI, j, nb * 512:nb * 512 + 512], qn[:, LO, j, nb * 512:nb * 512 + 512],
                                    j == 0, j == HC - 1)
                    last.then_inc(out_ready, 1)
                    if o == 1 and nb:
                        if nb == 3:
                            pe.wait_ge(ss_used, a.at(4, 1))
                        elif f:
                            pe.wait_ge(fin_done, f.at(8, 6 + nb))
                        elif nb == 1:
                            pe.wait_ge(m_read, a.at(4, 4))
                        norms(a, nb - 1)

            pe.wait_ge(w_lo, W_PARTS)
            turns(pe, body)


CX_AT, BD_AT, MM_AT, M_AT = 5, 7, 8, 10


def kt_bank(kg):
    return (kg + KT_LAG) % 2 if kg < 9 else 0


def kernel(x, ctx_4096, L0_xattn_Wq, L0_xattn_Wk, L0_xattn_Wv, L0_xattn_Wo, L0_xattn_bo, L0_xattn_g,
           L0_ffn_gate_w, L0_ffn_lora_A, L0_ffn_lora_B):
    import numpy as np
    import concourse.bacc as bacc
    from concourse import mybir as mb
    from concourse.bass_utils import run_bass_kernel_spmd

    def chunks(w):
        k, m = w.shape
        return np.ascontiguousarray(w.reshape(k // P, P, m).transpose(1, 0, 2).reshape(P, -1))

    arr = {k: np.asarray(v) for k, v in dict(
        x=x, ctx=ctx_4096, wq=L0_xattn_Wq, wk=L0_xattn_Wk, wv=L0_xattn_Wv, wo=L0_xattn_Wo, bo=L0_xattn_bo,
        g=L0_xattn_g, gate=L0_ffn_gate_w, la=L0_ffn_lora_A, lb=L0_ffn_lora_B).items()}
    n = arr["x"].shape[2]
    ins = {
        "x": np.ascontiguousarray(arr["x"]),
        "ctx": np.ascontiguousarray(arr["ctx"]),
        "wqT": chunks(arr["wq"].T), "wkT": chunks(arr["wk"].T), "wvT": chunks(arr["wv"].T),
        "woT": chunks(arr["wo"].T),
        "bo": np.ascontiguousarray(arr["bo"].reshape(-1, P).T),
        "g": np.ascontiguousarray(arr["g"].reshape(-1, P).T),
        "gateT": chunks(arr["gate"].T).reshape(P, n // P, E_N),
        "aT": chunks(arr["la"].reshape(-1, n).T),
        "bT": chunks(arr["lb"].transpose(0, 2, 1).reshape(-1, n)),
    }
    nc = bacc.Bacc("TRN2", target_bir_lowering=False, num_devices=1, dynamic_dma_scratch_size=1024)
    args = [nc.dram_tensor(f"in_{k}", a.shape, mb.dt.from_np(a.dtype), kind="ExternalInput").ap() for k, a in ins.items()]
    out = nc.dram_tensor("out_0", arr["x"].shape, mb.dt.float32, kind="ExternalOutput").ap()
    build(nc, *args, out)
    r = run_bass_kernel_spmd(nc, [{f"in_{k}": a for k, a in ins.items()}], core_ids=[0])
    return r.results[0]["out_0"]
```

```python
from contextlib import ExitStack

import concourse.bass as bass
from concourse import mybir

F32, F16, BF16, U32 = mybir.dt.float32, mybir.dt.float16, mybir.dt.bfloat16, mybir.dt.uint32
ALU = mybir.AluOpType
ACT = mybir.ActivationFunctionType
X = mybir.AxisListType.X

P = 128
HI, LO = 0, 1
HEADS, DH, E_N = 8, 64, 8

S_Z = 2.0**8
S_W = 2.0**6
S_C = 2.0**4
S_K = 2.0**12
S_M = 2.0**8
S_Q = 2.0**10
S_H = 2.0**5
S_N = 2.0**20

LN_EPS = 1e-5
NORM_FLOOR = 1e-12

RING = [5, 0, 4, 3]
Q_RING = [3, 0, 4]
PAIR = [1, 2]
GATE_BANK = RING[1]
KC_BANK = [4, 5]
M_BANK = 5
KT_LAG = 7
Q_LAG = 4


class Turn:

    def __init__(self, reg, off):
        self.reg, self.off = reg, off

    def at(self, per, k):
        const = self.off * per + k
        return const if self.reg is None else self.reg * per + const

    @property
    def index(self):
        return self.off if self.reg is None else self.reg + self.off

    @property
    def next(self):
        return Turn(self.reg, self.off + 1)


def build(nc, x, ctx, wqT, wkT, wvT, woT, bo, g, gateT, aT, bT, out):
    B, DIM, N = x.shape
    HID = HEADS * DH
    CC = DIM // P
    HC = HID // P
    NB = N // 512
    NT = N // P
    KTILES = HC * NB
    GROUPS = NT // 2
    assert (B, DIM, N, HID) == (16, 256, 2048, 512)

    x_v = x.rearrange("b (c p) n -> b p c n", p=P)
    c_v = ctx.rearrange("b (c p) n -> b p c n", p=P)
    o_v = out.rearrange("b (c p) n -> b p c n", p=P)

    es = ExitStack()
    with es:
        def sb(name, shape, dt):
            return es.enter_context(nc.sbuf_tensor(name, shape, dt))

        def sem(name):
            return es.enter_context(nc.semaphore(name))

        wq = sb("wq", [P, 2, CC, HID], F16)
        wk = sb("wk", [P, 2, CC, HID], F16)
        wv = sb("wv", [P, 2, CC, HID], F16)
        wo = sb("wo", [P, 2, HC, DIM], F16)
        wa = sb("wa", [P, 2, NT, HID], F16)
        wb = sb("wb", [P, 2, HC, N], F16)
        wg = sb("wg", [P, NT, 2 * E_N], F16)
        wg_raw = sb("wg_raw", [P, NT, E_N], F32)
        ones = sb("ones", [P, P], F32)
        ident = sb("ident", [P, P], F32)
        ident16 = sb("ident16", [P, P], F16)
        minus1 = sb("minus1", [P, P], BF16)
        pairmask = sb("pairmask", [P, P], F32)
        experts = sb("experts", [P, E_N], F32)
        minus_half = sb("minus_half", [P, CC], F32)
        bo_c = sb("bo_c", [P, CC], F32)
        g_c = sb("g_c", [P, CC], F32)

        stage = sb("stage", [P, CC, N], F32)
        xres = sb("xres", [P, CC, N], F32)
        opnd = sb("opnd", [P, 2, CC, N], F16)
        ct_m = sb("ct_m", [P, 2 * NT * DIM], F16)
        yz = sb("yz", [P, CC, N], F32)
        zt = sb("zt", [P, 2 * 2 * 512], F16)
        kq = sb("kq", [P, 2, NT * HID], F16)
        ke = sb("ke", [P, 8, 512], F32)
        kmx = sb("kmx", [P, HC, NB], F32)
        nkm = sb("nkm", [P, HC], F32)
        ksum = sb("ksum", [P, HC], F32)
        krcp = sb("krcp", [P, HC], F32)
        qmx = sb("qmx", [P, 4, HEADS], BF16)
        qsum = sb("qsum", [P, 4, HEADS], F32)
        qrcp = sb("qrcp", [P, 4, HEADS], F32)
        st1 = sb("st1", [P, CC, NB, 6], F32)
        st2 = sb("st2", [P, CC, NB, 6], F32)
        mv1 = sb("mv1", [P, CC, 2], F32)
        mv2 = sb("mv2", [P, CC, 2], F32)
        ve1 = sb("ve1", [P, CC], F32)
        ve2 = sb("ve2", [P, CC], F32)
        rs1 = sb("rs1", [P, CC], F32)
        rs2 = sb("rs2", [P, CC], F32)
        lgp = sb("lgp", [P, CC, 2 * E_N], F32)
        lg = sb("lg", [P, CC, E_N], F32)
        top = sb("top", [P, CC, 8], F32)
        who = sb("who", [P, CC, 8], U32)
        whof = sb("whof", [P, CC, 8], F32)
        gd = sb("gd", [P, CC], F32)
        ge = sb("ge", [P, CC], F32)
        gs = sb("gs", [P, CC], F32)
        gw = sb("gw", [P, 2, CC], F32)
        gpick = sb("gpick", [P, CC, 2, E_N], F32)
        carrier = sb("carrier", [P, 1], F32)
        gfull = sb("gfull", [P, CC, E_N], F32)

        kt = kq[:, :, :].rearrange("p h (n d) -> p h n d", d=HID)
        qn = kq[:, :, :].rearrange("p h (j n) -> p h j n", n=N)
        kraw = ke[:, :, :].rearrange("p (s t) n -> p s (t n)", s=2)
        sq = ke[:, :, :].rearrange("p (b o) n -> p b o n", o=2)
        ct = ct_m[:, :].rearrange("p (h n c) -> p h n c", h=2, n=NT)
        kc = ct_m[:, 0:2048].rearrange("p (h c d) -> p h c d", h=2, c=CC)
        bd = ct_m[:, 2048:3072].rearrange("p (h d) -> p h d", h=2)
        mm = ct_m[:, 3072:5120].rearrange("p (h j o) -> p h j o", h=2, j=HC)
        bdf = ct_m[:, 5120:6144].bitcast(F32)
        mf = ct_m[:, 6144:8192].bitcast(F32).rearrange("p (j o) -> p j o", j=HC)
        z2t = zt[:, :].rearrange("p (s h n t) -> p s h n t", s=2, h=2, n=2)
        hwt = zt[:, :].rearrange("p (h j t) -> p h j t", h=2, j=HC)
        hw = yz[:, 0, 0:CC * HID].rearrange("p (t d) -> p t d", t=CC)

        raw_w = wa[:, HI, :, :].rearrange("p n d -> p (n d)").bitcast(F32).rearrange("p (w n) -> p w n", w=4)
        raw_a = wb[:, :, :, :].rearrange("p h j n -> p (h j n)").bitcast(F32)
        raw_b = [yz[:, :, :].rearrange("p c n -> p (c n)"), xres[:, :, :].rearrange("p c n -> p (c n)")]

        ps = es.enter_context(nc.psum_tensor("ps", [P, 6, 512], F32))
        tp = es.enter_context(nc.psum_tensor("tp", [P, 2, 512], F32))

        w_in = [sem(f"w_in{i}") for i in range(4)]
        a_in, b_in, s_in = sem("a_in"), [sem("b_in0"), sem("b_in1")], sem("s_in")
        w_hi, w_lo = sem("w_hi"), sem("w_lo")
        consts, consts2, consts3 = sem("consts"), sem("consts2"), sem("consts3")
        ctx_in = [sem("ctx_in0"), sem("ctx_in1")]
        x_in = [sem("x_in0"), sem("x_in1")]
        res_in = sem("res_in")
        out_done = [sem("out_done0"), sem("out_done1")]
        ctx_hi, ctx_split = sem("ctx_hi"), sem("ctx_split")
        k_ready, k_copied = sem("k_ready"), sem("k_copied")
        k_max, k_exp = sem("k_max"), sem("k_exp")
        kmx_done = sem("kmx_done")
        ct_ready, ct_done = sem("ct_ready"), sem("ct_done")
        kt_ready, kt_hi, kt_done = sem("kt_ready"), sem("kt_hi"), sem("kt_done")
        st1_done, ln1_in, ln1_r = sem("st1_done"), sem("ln1_in"), sem("ln1_r")
        z1_f, z1_hi, z1_split = sem("z1_f"), sem("z1_hi"), sem("z1_split")
        kc_ready, kc_hi, kc_split = sem("kc_ready"), sem("kc_hi"), sem("kc_split")
        cx_ready, bd_f, bd_hi, bd_split = sem("cx_ready"), sem("bd_f"), sem("bd_hi"), sem("bd_split")
        kr_done = sem("kr_done")
        m_ready, m_read, m_hi, m_split = sem("m_ready"), sem("m_read"), sem("m_hi"), sem("m_split")
        q_ready, q_max, q_sub, q_exp = sem("q_ready"), sem("q_max"), sem("q_sub"), sem("q_exp")
        q_sum, q_rcp, q_nrm = sem("q_sum"), sem("q_rcp"), sem("q_nrm")
        qt_ready, qt_hi, qt_done = sem("qt_ready"), sem("qt_hi"), sem("qt_done")
        out_ready, out_y, out_used = sem("out_ready"), sem("out_y"), sem("out_used")
        sqs_ready, ss_ready, ss_used = sem("sqs_ready"), sem("ss_ready"), sem("ss_used")
        ln_done, rb_ready, t_done = sem("ln_done"), sem("rb_ready"), sem("t_done")
        x2_done = sem("x2_done")
        st2_done, ln2_in, ln2_r = sem("st2_done"), sem("ln2_in"), sem("ln2_r")
        z2_ready = sem("z2_ready")
        zt_ready, zt_hi, zt_done, zt_used = sem("zt_ready"), sem("zt_hi"), sem("zt_done"), sem("zt_used")
        ha_ready, gate_step, gate_exp = sem("ha_ready"), sem("gate_step"), sem("gate_exp")
        gate_read, hw_done = sem("gate_read"), sem("hw_done")
        ht_ready, ht_hi, ht_done = sem("ht_ready"), sem("ht_hi"), sem("ht_done")
        y_ready, fin_done = sem("y_ready"), sem("fin_done")
        G_STEPS = 15

        block = es.enter_context(nc.Block())

        def turns(eng, body):
            body(Turn(None, 0), None, True)
            with eng.Fori(0, B - 2) as i:
                body(Turn(i, 1), Turn(i, 0), True)
            body(Turn(None, B - 1), Turn(None, B - 2), False)
            body(None, Turn(None, B - 1), False)

        WEIGHTS = [(raw_w[:, i, :], w_in[i], w) for i, w in enumerate((
            wk[:, :, :, :].rearrange("p h c n -> p h (c n)"), wq[:, :, :, :].rearrange("p h c n -> p h (c n)"),
            wv[:, :, :, :].rearrange("p h c n -> p h (c n)"), wo[:, :, :, :].rearrange("p h c n -> p h (c n)")))]
        wa_f = wa[:, :, :, :].rearrange("p h c n -> p h (c n)")
        wb_f = wb[:, :, :, :].rearrange("p h c n -> p h (c n)")
        WEIGHTS.append((wg_raw[:, :, :], s_in, wg[:, :, :].rearrange("p c (h e) -> p h c e", h=2)))
        for i in range(4):
            WEIGHTS.append((raw_a[:, i * 2048:(i + 1) * 2048], a_in, wa_f[:, :, i * 2048:(i + 1) * 2048]))
        for i in range(4):
            WEIGHTS.append((raw_b[i // 2][:, (i % 2) * 2048:(i % 2 + 1) * 2048], b_in[i // 2],
                            wb_f[:, :, i * 2048:(i + 1) * 2048]))
        W_PARTS, A_PART, B_PARTS = len(WEIGHTS), 5, 4

        @block.sync
        def _(sp):
            def load_ctx(a):
                for c in range(CC):
                    sp.dma_start(stage[:, c, :], c_v[a.index, :, c, :]).then_inc(ctx_in[c], 16)

            def load_x(a):
                for c in range(CC):
                    sp.wait_ge(ctx_split, a.at(2, c + 1))
                    sp.dma_start(stage[:, c, :], x_v[a.index, :, c, :]).then_inc(x_in[c], 16)

            load_ctx(Turn(None, 0))
            for i, w in enumerate((wkT, wqT, wvT, woT)):
                sp.dma_start(raw_w[:, i, :], w).then_inc(w_in[i], 16)
            for dst, src in ((wg_raw[:, :, :], gateT), (bo_c[:, :], bo), (g_c[:, :], g)):
                sp.dma_start(dst, src).then_inc(s_in, 16)
            load_x(Turn(None, 0))
            sp.dma_start(raw_a, aT).then_inc(a_in, 16)
            for i in range(2):
                sp.dma_start(raw_b[i], bT[:, i * 4096:(i + 1) * 4096]).then_inc(b_in[i], 16)

            def body(a, f, more):
                if more:
                    for c in range(CC):
                        sp.wait_ge(z1_split, a.at(2, c + 1))
                        sp.dma_start(stage[:, c, :], c_v[a.next.index, :, c, :]).then_inc(ctx_in[c], 16)
                if f:
                    for c in range(CC):
                        sp.wait_ge(fin_done, f.at(8, 4 * c + 4))
                        sp.dma_start(o_v[f.index, :, c, :], xres[:, c, :]).then_inc(out_done[c], 16)
                    for c in range(CC):
                        sp.wait_ge(out_done[c], f.at(16, 16))
                else:
                    sp.wait_ge(w_lo, W_PARTS)
                if a:
                    sp.dma_start(xres[:, :, :], x_v[a.index]).then_inc(res_in, 16)
                if more:
                    load_x(a.next)

            turns(sp, body)

        @block.gpsimd
        def _(pool):
            nc.gpsimd.memset(ident[:, :], 0.0).then_inc(consts, 1)
            nc.gpsimd.memset(ones[:, :], 1.0).then_inc(consts, 1)
            nc.gpsimd.memset(minus_half[:, :], -0.5).then_inc(consts, 1)
            for e in range(E_N):
                nc.gpsimd.memset(experts[:, e:e + 1], float(e)).then_inc(consts, 1)
            pool.wait_ge(consts, 11)
            nc.gpsimd.affine_select(out=ident[:, :], in_=ident[:, :], compare_op=ALU.not_equal, fill=1.0,
                                    base=0, pattern=[[-1, P]], channel_multiplier=1).then_inc(consts, 1)

            def body(a, f, more):
                if f:
                    add_x(f, 2)
                    add_x(f, 3)
                    pool.wait_ge(ln2_in, f.at(3, 3))
                    nc.gpsimd.tensor_tensor(rs2[:, :], ve2[:, :], minus_half[:, :], ALU.pow).then_inc(ln2_r, 1)
                if a:
                    pool.wait_ge(ln1_in, a.at(3, 3))
                    nc.gpsimd.tensor_tensor(rs1[:, :], ve1[:, :], minus_half[:, :], ALU.pow).then_inc(ln1_r, 1)
                    for i in range(NT):
                        pool.wait_ge(q_rcp, a.at(16, i + 1))
                        e = ke[:, i % 8, :].rearrange("p (h d) -> p h d", h=HEADS)
                        r = qrcp[:, i % 4, :].unsqueeze(2).to_broadcast([P, HEADS, DH])
                        nc.gpsimd.tensor_tensor(e, e, r, ALU.mult).then_inc(q_nrm, 1)
                    pool.wait_ge(res_in, a.at(16, 16))
                    add_x(a, 0)
                    add_x(a, 1)

            def add_x(t, nb):
                pool.wait_ge(t_done, t.at(8, 2 * nb + 2))
                cols = slice(nb * 512, nb * 512 + 512)
                nc.gpsimd.tensor_tensor(xres[:, :, cols], xres[:, :, cols], yz[:, :, cols],
                                        ALU.add).then_inc(x2_done, 1)

            turns(pool, body)

        @block.scalar
        def _(act):
            def split_ctx(a):
                for c in range(CC):
                    act.wait_ge(ctx_in[c], a.at(16, 16))
                    nc.scalar.activation(opnd[:, HI, c, :], stage[:, c, :], ACT.Copy, scale=S_C).then_inc(ctx_hi, 1)

            def split_weight(i):
                raw, landed, parts = WEIGHTS[i]
                act.wait_ge(landed, 48 if landed is s_in else 16)
                if i == A_PART:
                    act.wait_ge(w_lo, A_PART - 1)
                if i >= W_PARTS - B_PARTS:
                    act.wait_ge(w_lo, W_PARTS - B_PARTS)
                nc.scalar.activation(parts[:, HI, :], raw, ACT.Copy, scale=S_W).then_inc(w_hi, 1)

            nc.scalar.preload_act_table_set("natural_log_exp_and_others")
            split_ctx(Turn(None, 0))
            split_weight(0)

            def exp_k(a, j):
                act.wait_ge(k_max, a.at(4, j + 1))
                nc.scalar.activation(kraw[:, j % 2, :], kraw[:, j % 2, :], ACT.Exp, bias=nkm[:, j:j + 1],
                                     accum_out=ksum[:, j:j + 1]).then_inc(k_exp, 1)

            def kt_high(a, kg):
                act.wait_ge(kt_ready, a.at(16, kg + 1))
                j, t = kg // 4, kg % 4
                src = tp[:, kt_bank(kg), :].rearrange("p (n d) -> p n d", n=4)
                nc.scalar.activation(kt[:, HI, 4 * t:4 * t + 4, j * P:(j + 1) * P], src, ACT.Copy,
                                     scale=S_K).then_inc(kt_hi, 1)

            def row_scale(t, nb):
                act.wait_ge(ss_used, t.at(4, nb + 1))
                nc.scalar.activation(sq[:, nb, 1, :], sq[:, nb, 1, :], ACT.Ln, scale=S_N).then_inc(ln_done, 1)
                act.wait_ge(ln_done, t.at(4, nb + 1))
                nc.scalar.activation(sq[:, nb, 1, :], sq[:, nb, 1, :], ACT.Exp, scale=-0.5).then_inc(rb_ready, 1)

            def body(a, f, more):
                for i in range(KTILES if a else 0):
                    if f and i % 4 == 0 and i < 8:
                        act.wait_ge(t_done, f.at(8, 4 + i))
                    act.wait_ge(k_ready, a.at(16, i + 1))
                    nc.scalar.activation(ke[:, i % 8, :], ps[:, RING[i % 4], :], ACT.Copy,
                                         scale=1.0 / (S_C * S_W)).then_inc(k_copied, 1)
                    if f and i == 2:
                        row_scale(f, 3)
                    if i % 4 == 1 and i > 4:
                        exp_k(a, i // 4 - 1)
                    if i % 2:
                        act.wait_ge(ct_ready, a.at(8, i // 2 + 1))
                        src = tp[:, 0, :].bitcast(F16).rearrange("p (h n c) -> p h n c", h=2, n=2)
                        nc.scalar.activation(ct[:, :, i - 1:i + 1, :], src, ACT.Copy).then_inc(ct_done, 1)
                    if i >= KT_LAG:
                        kt_high(a, i - KT_LAG)
                if f and not a:
                    row_scale(f, 3)
                if a:
                    exp_k(a, 3)
                if not f:
                    for i in range(1, A_PART):
                        split_weight(i)
                for gr in range(GROUPS):
                    if f:
                        act.wait_ge(zt_ready, f.at(8, gr + 1))
                        if gr >= 2:
                            act.wait_ge(zt_used, f.at(GROUPS - 1, gr - 1))
                        nc.scalar.activation(z2t[:, gr % 2, HI, :, :], tp[:, 1, :].rearrange("p (n t) -> p n t", n=2),
                                             ACT.Copy, scale=S_Z).then_inc(zt_hi, 1)
                    if a and 9 + gr < KTILES:
                        kt_high(a, 9 + gr)
                if a:
                    act.wait_ge(ct_ready, a.at(8, 8))
                    for c in range(CC):
                        act.wait_ge(z1_f, a.at(2, c + 1))
                        nc.scalar.activation(opnd[:, HI, c, :], stage[:, c, :], ACT.Copy, scale=S_Z).then_inc(z1_hi, 1)
                if not f:
                    for i in range(A_PART, W_PARTS - B_PARTS):
                        split_weight(i)
                if f:
                    act.wait_ge(gate_step, f.at(G_STEPS, G_DIFF))
                    nc.scalar.activation(ge[:, :], gd[:, :], ACT.Exp).then_inc(gate_exp, 1)
                if a:
                    for c in range(CC):
                        act.wait_ge(kc_ready, a.at(2, c + 1))
                        nc.scalar.activation(kc[:, HI, c, :], ps[:, KC_BANK[c], :], ACT.Copy,
                                             scale=1.0 / (S_K * S_C)).then_inc(kc_hi, 1)
                if f:
                    for t in range(CC):
                        act.wait_ge(ht_ready, f.at(2, t + 1))
                        nc.scalar.activation(hwt[:, HI, :, t * P:(t + 1) * P],
                                             tp[:, t, :].rearrange("p (j n) -> p j n", j=HC), ACT.Copy).then_inc(ht_hi, 1)
                for s in range(1, NT + Q_LAG if a else 0):
                    if s <= NT:
                        act.wait_ge(q_sub, a.at(16, s))
                        nc.scalar.activation(ke[:, (s - 1) % 8, :], ps[:, Q_RING[(s - 1) % 3], :], ACT.Exp,
                                             scale=1.0 / (S_Z * S_W)).then_inc(q_exp, 1)
                    if s == BD_AT:
                        act.wait_ge(bd_f, a.at(1, 1))
                        nc.scalar.activation(bd[:, HI, :], bdf, ACT.Copy).then_inc(bd_hi, 1)
                    if s == M_AT:
                        act.wait_ge(m_read, a.at(4, 4))
                        nc.scalar.activation(mm[:, HI, :, :], mf, ACT.Copy).then_inc(m_hi, 1)
                    if not f and 1 <= s <= B_PARTS:
                        split_weight(W_PARTS - B_PARTS + s - 1)
                    if s >= Q_LAG:
                        i = s - Q_LAG
                        act.wait_ge(qt_ready, a.at(16, i + 1))
                        nc.scalar.activation(qn[:, HI, :, i * P:(i + 1) * P],
                                             tp[:, i % 2, :].rearrange("p (j n) -> p j n", j=HC),
                                             ACT.Copy, scale=S_Q).then_inc(qt_hi, 1)
                    if more and s == NT + 1:
                        act.wait_ge(q_ready, a.at(16, 16))
                        split_ctx(a.next)
                if not f:
                    act.wait_ge(w_lo, W_PARTS)
                for nb in range(NB if a else 0):
                    for o in range(CC):
                        i = nb * CC + o
                        act.wait_ge(out_ready, a.at(8, i + 1))
                        tile = ps[:, RING[i % 4], :]
                        nc.scalar.activation(yz[:, o, nb * 512:nb * 512 + 512], tile, ACT.Identity,
                                             bias=bo_c[:, o:o + 1], scale=DH**-0.5 / (S_M * S_Q)).then_inc(out_y, 1)
                        nc.scalar.activation(sq[:, nb, o, :], tile, ACT.Square,
                                             bias=bo_c[:, o:o + 1], scale=DH**-0.5 / (S_M * S_Q)).then_inc(out_used, 1)
                    if nb:
                        row_scale(a, nb - 1)

            G_DIFF = 7
            turns(act, body)

        @block.vector
        def _(dve):
            def low(out_, raw, scale, high):
                return nc.vector.scalar_tensor_tensor(out=out_, in0=raw, scalar=scale, in1=high,
                                                      op0=ALU.mult, op1=ALU.subtract)

            def split_ctx(a):
                for c in range(CC):
                    dve.wait_ge(ctx_hi, a.at(2, c + 1))
                    low(opnd[:, LO, c, :], stage[:, c, :], S_C, opnd[:, HI, c, :]).then_inc(ctx_split, 1)

            def split_weight(i):
                raw, _, parts = WEIGHTS[i]
                dve.wait_ge(w_hi, i + 1)
                low(parts[:, LO, :], raw, S_W, parts[:, HI, :]).then_inc(w_lo, 1)

            split_ctx(Turn(None, 0))
            split_weight(0)
            nc.vector.memset(pairmask[:, :], 0.0).then_inc(consts3, 1)
            dve.wait_ge(consts3, 1)
            nc.vector.memset(pairmask[0:DH, 0:DH], 1.0).then_inc(consts3, 1)
            nc.vector.memset(pairmask[DH:P, DH:P], 1.0).then_inc(consts3, 1)
            dve.wait_ge(consts, 12)
            nc.vector.tensor_copy(ident16[:, :], ident[:, :]).then_inc(consts2, 1)
            nc.vector.tensor_scalar(minus1[:, :], ident[:, :], -1.0, None, ALU.mult).then_inc(consts2, 1)
            dve.wait_ge(consts2, 2)
            dve.wait_ge(consts3, 3)

            def carry():
                nc.vector.memset(carrier[:, :], 0.0)

            def max_k(a, i):
                dve.wait_ge(k_copied, a.at(16, i + 1))
                nc.vector.reduce_max(kmx[:, i // 4, i % 4:i % 4 + 1], ke[:, i % 8, :], X).then_inc(kmx_done, 1)
                if i % 4 == 3:
                    dve.wait_ge(kmx_done, a.at(16, i + 1))
                    nc.vector.tensor_reduce(nkm[:, i // 4:i // 4 + 1], kmx[:, i // 4, :], X, ALU.max,
                                            negate=True).then_inc(k_max, 1)

            def kt_low(a, kg):
                dve.wait_ge(kt_hi, a.at(16, kg + 1))
                j, t = kg // 4, kg % 4
                src = tp[:, kt_bank(kg), :].rearrange("p (n d) -> p n d", n=4)
                where = (slice(4 * t, 4 * t + 4), slice(j * P, (j + 1) * P))
                low(kt[:, LO, where[0], where[1]], src, S_K, kt[:, HI, where[0], where[1]]).then_inc(kt_done, 1)

            def floor_norm(t, nb):
                dve.wait_ge(ss_ready, t.at(4, nb + 1))
                nc.vector.tensor_scalar(sq[:, nb, 1, :], ps[:, PAIR[nb % 2], :], NORM_FLOOR**2, None,
                                        ALU.max).then_inc(ss_used, 1)

            def scale_y(t, nb):
                dve.wait_ge(rb_ready, t.at(4, nb + 1))
                for o in range(CC):
                    y = yz[:, o, nb * 512:nb * 512 + 512]
                    nc.vector.scalar_tensor_tensor(out=y, in0=y, scalar=g_c[:, o:o + 1], in1=sq[:, nb, 1, :],
                                                   op0=ALU.mult, op1=ALU.mult).then_inc(t_done, 1)

            def stats2(f, nb):
                dve.wait_ge(x2_done, f.at(4, nb + 1))
                for o in range(CC):
                    nc.vector.bn_stats(st2[:, o, nb, :], xres[:, o, nb * 512:nb * 512 + 512]).then_inc(st2_done, 1)

            def mean_var(t, st_done, st, mv, ve, ln_in):
                dve.wait_ge(st_done, t.at(8, 8))
                carry()
                for o in range(CC):
                    nc.vector.bn_aggr(mv[:, o, :], st[:, o, :, :].rearrange("p b s -> p (b s)")).then_inc(ln_in, 1)
                dve.wait_ge(ln_in, t.at(3, 2))
                nc.vector.tensor_scalar(ve[:, :], mv[:, :, 1], LN_EPS, None, ALU.add).then_inc(ln_in, 1)

            def z2_rows(f, o):
                if o == 0:
                    dve.wait_ge(ln2_r, f.at(1, 1))
                nc.vector.tensor_scalar(yz[:, o, :], xres[:, o, :], mv2[:, o, 0:1], rs2[:, o:o + 1],
                                        ALU.subtract, ALU.mult).then_inc(z2_ready, 1)

            def gate(f):
                n = [0]

                def step(ins, wait=True):
                    n[0] += 1
                    ins.then_inc(gate_step, 1)
                    if wait:
                        dve.wait_ge(gate_step, f.at(G_STEPS, n[0]))

                dve.wait_ge(ha_ready, f.at(1, 1))
                nc.vector.tensor_scalar(lgp[:, :, :], ps[:, GATE_BANK, 0:CC * 2 * E_N].rearrange("p (t e) -> p t e", t=CC),
                                        1.0 / (S_Z * S_W), None, ALU.mult).then_inc(gate_read, 1)
                dve.wait_ge(gate_read, f.at(1, 1))
                step(nc.vector.tensor_tensor(lg[:, :, :], lgp[:, :, 0:E_N], lgp[:, :, E_N:2 * E_N], ALU.add))
                carry()
                step(nc.vector.max(top[:, 0, :], lg[:, 0, :]), False)
                step(nc.vector.max(top[:, 1, :], lg[:, 1, :]), False)
                dve.wait_ge(gate_step, f.at(G_STEPS, 3))
                carry()
                step(nc.vector.max_index(who[:, 0, :], top[:, 0, :], lg[:, 0, :]), False)
                step(nc.vector.max_index(who[:, 1, :], top[:, 1, :], lg[:, 1, :]))
                step(nc.vector.tensor_copy(whof[:, :, :], who[:, :, :]), False)
                step(nc.vector.tensor_tensor(gd[:, :], top[:, :, 1], top[:, :, 0], ALU.subtract))
                dve.wait_ge(gate_exp, f.at(1, 1))
                step(nc.vector.tensor_scalar(gs[:, :], ge[:, :], 1.0, None, ALU.add))
                step(nc.vector.reciprocal(gw[:, 0, :], gs[:, :]))
                step(nc.vector.tensor_tensor(gw[:, 1, :], ge[:, :], gw[:, 0, :], ALU.mult))
                for t in range(CC):
                    for r in range(2):
                        step(nc.vector.tensor_scalar(gpick[:, t, r, :], experts[:, :], whof[:, t, r:r + 1],
                                                     gw[:, r, t:t + 1], ALU.is_equal, ALU.mult), t + r == 2)
                step(nc.vector.tensor_tensor(gfull[:, :, :], gpick[:, :, 0, :], gpick[:, :, 1, :], ALU.add))
                assert n[0] == G_STEPS
                for t in range(CC):
                    nc.vector.scalar_tensor_tensor(
                        out=hw[:, t, :].rearrange("p (e r) -> p e r", e=E_N),
                        in0=ps[:, PAIR[t], :].rearrange("p (e r) -> p e r", e=E_N), scalar=S_H / (S_Z * S_W),
                        in1=gfull[:, t, :].unsqueeze(2).to_broadcast([P, E_N, DH]),
                        op0=ALU.mult, op1=ALU.mult).then_inc(hw_done, 1)

            def body(a, f, more):
                tail = {}
                if f:
                    tail = {0: [(scale_y, 2)], 1: [(floor_norm, 3), (stats2, 0)], 2: [(stats2, 1)],
                            3: [(scale_y, 3)], 4: [(stats2, 2)], 6: [(stats2, 3)]}
                for i in range(KTILES):
                    if a:
                        max_k(a, i)
                        if i >= KT_LAG:
                            kt_low(a, i - KT_LAG)
                    for what, nb in tail.get(i, []):
                        what(f, nb)
                    if f and i == 7:
                        mean_var(f, st2_done, st2, mv2, ve2, ln2_in)
                    if f and i in (9, 10):
                        z2_rows(f, i - 9)
                for gr in range(GROUPS):
                    if f:
                        dve.wait_ge(zt_hi, f.at(8, gr + 1))
                        low(z2t[:, gr % 2, LO, :, :], tp[:, 1, :].rearrange("p (n t) -> p n t", n=2), S_Z,
                            z2t[:, gr % 2, HI, :, :]).then_inc(zt_done, 1)
                    if a and 9 + gr < KTILES:
                        kt_low(a, 9 + gr)
                    if a:
                        o, nb = gr // NB, gr % NB
                        if nb == 0:
                            dve.wait_ge(x_in[o], a.at(16, 16))
                        nc.vector.bn_stats(st1[:, o, nb, :], stage[:, o, nb * 512:nb * 512 + 512]).then_inc(st1_done, 1)
                if not f:
                    for i in range(1, A_PART):
                        split_weight(i)
                    dve.wait_ge(s_in, 48)
                    nc.vector.tensor_scalar(g_c[:, :], g_c[:, :], DIM**0.5 * S_N**0.5, None, ALU.mult).then_inc(consts2, 1)
                    dve.wait_ge(consts2, 3)
                if a:
                    mean_var(a, st1_done, st1, mv1, ve1, ln1_in)
                    dve.wait_ge(ln1_r, a.at(1, 1))
                    for o in range(CC):
                        nc.vector.tensor_scalar(stage[:, o, :], stage[:, o, :], mv1[:, o, 0:1], rs1[:, o:o + 1],
                                                ALU.subtract, ALU.mult).then_inc(z1_f, 1)
                    for o in range(CC):
                        dve.wait_ge(z1_hi, a.at(2, o + 1))
                        low(opnd[:, LO, o, :], stage[:, o, :], S_Z, opnd[:, HI, o, :]).then_inc(z1_split, 1)
                    dve.wait_ge(k_exp, a.at(4, 4))
                    nc.vector.reciprocal(krcp[:, :], ksum[:, :]).then_inc(kr_done, 1)
                if f:
                    gate(f)
                else:
                    for i in range(A_PART, W_PARTS - B_PARTS):
                        split_weight(i)
                if a:
                    for c in range(CC):
                        dve.wait_ge(kc_hi, a.at(2, c + 1))
                        low(kc[:, LO, c, :], ps[:, KC_BANK[c], :], 1.0 / (S_K * S_C), kc[:, HI, c, :]).then_inc(kc_split, 1)
                if f:
                    for t in range(CC):
                        dve.wait_ge(ht_hi, f.at(2, t + 1))
                        low(hwt[:, LO, :, t * P:(t + 1) * P], tp[:, t, :].rearrange("p (j n) -> p j n", j=HC), 1.0,
                            hwt[:, HI, :, t * P:(t + 1) * P]).then_inc(ht_done, 1)
                for s in range(NT + Q_LAG + 1):
                    if a and s >= Q_LAG + 1:
                        i = s - Q_LAG - 1
                        dve.wait_ge(qt_hi, a.at(16, i + 1))
                        cols = slice(i * P, (i + 1) * P)
                        low(qn[:, LO, :, cols], tp[:, i % 2, :].rearrange("p (j n) -> p j n", j=HC), S_Q,
                            qn[:, HI, :, cols]).then_inc(qt_done, 1)
                    if a and s < NT:
                        dve.wait_ge(q_ready, a.at(16, s + 1))
                        nc.vector.reduce_max(qmx[:, s % 4, :],
                                             ps[:, Q_RING[s % 3], :].rearrange("p (h d) -> p h d", h=HEADS),
                                             X).then_inc(q_max, 1)
                    if a and 1 <= s <= NT:
                        i = s - 1
                        dve.wait_ge(q_exp, a.at(16, i + 1))
                        if i >= 4:
                            dve.wait_ge(q_nrm, a.at(16, i - 3))
                        nc.vector.reduce_sum(qsum[:, i % 4, :], ke[:, i % 8, :].rearrange("p (h d) -> p h d", h=HEADS),
                                             X).then_inc(q_sum, 1)
                        dve.wait_ge(q_sum, a.at(16, i + 1))
                        nc.vector.reciprocal(qrcp[:, i % 4, :], qsum[:, i % 4, :]).then_inc(q_rcp, 1)
                    if a and s == CX_AT + 1:
                        dve.wait_ge(cx_ready, a.at(1, 1))
                        nc.vector.scalar_tensor_tensor(
                            out=bdf.rearrange("p (j d) -> p j d", j=HC),
                            in0=ps[:, M_BANK, :].rearrange("p (j d) -> p j d", j=HC), scalar=1.0 / S_W,
                            in1=pairmask[:, :].unsqueeze(1).to_broadcast([P, HC, P]),
                            op0=ALU.mult, op1=ALU.mult).then_inc(bd_f, 1)
                    if a and s == BD_AT:
                        dve.wait_ge(bd_hi, a.at(1, 1))
                        nc.vector.tensor_tensor(bd[:, LO, :], bdf, bd[:, HI, :], ALU.subtract).then_inc(bd_split, 1)
                    if a and s in (MM_AT[0] + 1, MM_AT[1] + 1):
                        half = MM_AT.index(s - 1)
                        dve.wait_ge(kr_done, a.at(1, 1))
                        dve.wait_ge(m_ready, a.at(2, half + 1))
                        for j in (2 * half, 2 * half + 1):
                            nc.vector.tensor_scalar(mf[:, j, :], ps[:, M_BANK, (j % 2) * DIM:(j % 2 + 1) * DIM],
                                                    krcp[:, j:j + 1], S_M / S_W, ALU.mult, ALU.mult).then_inc(m_read, 1)
                    if a and s == M_AT:
                        dve.wait_ge(m_hi, a.at(1, 1))
                        nc.vector.tensor_tensor(mm[:, LO, :, :], mf, mm[:, HI, :, :], ALU.subtract).then_inc(m_split, 1)
                    if not f and 1 <= s <= B_PARTS:
                        split_weight(W_PARTS - B_PARTS + s - 1)
                    if f and s >= Y_AT + 2 and (s - Y_AT) % 2 == 0 and s < Y_AT + 18:
                        u = (s - Y_AT) // 2 - 1
                        t, nb = u // NB, u % NB
                        dve.wait_ge(y_ready, f.at(8, u + 1))
                        acc = xres[:, t, nb * 512:nb * 512 + 512]
                        nc.vector.scalar_tensor_tensor(out=acc, in0=ps[:, PAIR[u % 2], :], scalar=1.0 / (S_H * S_W),
                                                       in1=acc, op0=ALU.mult, op1=ALU.add).then_inc(fin_done, 1)
                    if more and s == NT + 2:
                        split_ctx(a.next)
                for nb in range(NB if a else 0):
                    dve.wait_ge(out_used, a.at(8, 2 * nb + 2))
                    nc.vector.tensor_tensor(sq[:, nb, 0, :], sq[:, nb, 0, :], sq[:, nb, 1, :], ALU.add).then_inc(sqs_ready, 1)
                    if nb >= 1:
                        floor_norm(a, nb - 1)
                    if nb >= 2:
                        scale_y(a, nb - 2)

            turns(dve, body)

        @block.tensor
        def _(pe):
            def mac3(acc, l_hi, l_lo, r_hi, r_lo, first, last):
                nc.tensor.matmul(acc, l_hi, r_hi, start=first, stop=False)
                nc.tensor.matmul(acc, l_hi, r_lo, start=False, stop=False)
                return nc.tensor.matmul(acc, l_lo, r_hi, start=False, stop=last)

            pe.wait_ge(consts2, 2)

            def norms(t, nb):
                pe.wait_ge(sqs_ready, t.at(4, nb + 1))
                nc.tensor.matmul(ps[:, PAIR[nb % 2], :], ones[:, :], sq[:, nb, 0, :],
                                 start=True, stop=True).then_inc(ss_ready, 1)

            def kt_blocks(a, kg):
                j, t = kg // 4, kg % 4
                if t == 0:
                    pe.wait_ge(k_exp, a.at(4, j + 1))
                for q in range(4):
                    n = 4 * t + q
                    last = nc.tensor.transpose(tp[:, kt_bank(kg), q * P:(q + 1) * P],
                                               kraw[:, j % 2, n * P:(n + 1) * P], ident[:, :])
                last.then_inc(kt_ready, 1)

            def body(a, f, more):
                for i in range(KTILES if a else 0):
                    j, nb = i // NB, i % NB
                    if i == 0:
                        if not f:
                            pe.wait_ge(w_lo, 1)
                        pe.wait_ge(ctx_split, a.at(2, 2))
                    if i >= 4:
                        pe.wait_ge(k_copied, a.at(16, i - 3))
                    elif f:
                        pe.wait_ge(out_used, f.at(8, 5 + i))
                    acc = ps[:, RING[i % 4], :]
                    for c in range(CC):
                        last = mac3(acc, wk[:, HI, c, j * P:(j + 1) * P], wk[:, LO, c, j * P:(j + 1) * P],
                                    opnd[:, HI, c, nb * 512:nb * 512 + 512], opnd[:, LO, c, nb * 512:nb * 512 + 512],
                                    c == 0, c == CC - 1)
                    last.then_inc(k_ready, 1)
                    if f and i == 1:
                        pe.wait_ge(ss_used, f.at(4, 2))
                        norms(f, 3)
                    if i % 2:
                        m = i // 2
                        if i - 1 >= KT_LAG:
                            pe.wait_ge(kt_done, a.at(16, i - KT_LAG))
                        elif m:
                            pe.wait_ge(ct_done, a.at(8, m))
                        dst = tp[:, 0, :].bitcast(F16).rearrange("p (h n c) -> p h n c", h=2, n=2)
                        for h in range(2):
                            for q in range(2):
                                for c in range(CC):
                                    n = 2 * m + q
                                    last = nc.tensor.transpose(dst[:, h, q, c * P:(c + 1) * P],
                                                               opnd[:, h, c, n * P:(n + 1) * P], ident16[:, :])
                        last.then_inc(ct_ready, 1)
                    if i >= KT_LAG:
                        kg = i - KT_LAG
                        if i % 2 == 0:
                            pe.wait_ge(ct_done, a.at(8, i // 2))
                        elif kg >= 2:
                            pe.wait_ge(kt_done, a.at(16, kg - 1))
                        kt_blocks(a, kg)
                if f and not a:
                    pe.wait_ge(ss_used, f.at(4, 2))
                    norms(f, 3)

                def z2_blocks(gr):
                    for q in range(2):
                        for t in range(CC):
                            n = 2 * gr + q
                            last = nc.tensor.transpose(tp[:, 1, (q * CC + t) * P:(q * CC + t + 1) * P],
                                                       yz[:, t, n * P:(n + 1) * P], ident[:, :])
                    last.then_inc(zt_ready, 1)

                if f:
                    if a:
                        pe.wait_ge(kt_done, a.at(16, 9))
                    pe.wait_ge(z2_ready, f.at(2, 2))
                    z2_blocks(0)
                for gr in range(GROUPS):
                    if a and 9 + gr < KTILES:
                        if gr == 0:
                            pe.wait_ge(ct_done, a.at(8, 8))
                        else:
                            pe.wait_ge(kt_done, a.at(16, 9 + gr))
                        kt_blocks(a, 9 + gr)
                    if not f:
                        continue
                    pe.wait_ge(zt_done, f.at(8, gr + 1))
                    if gr + 1 < GROUPS:
                        z2_blocks(gr + 1)
                    if gr == 0:
                        if a:
                            pe.wait_ge(k_copied, a.at(16, 14))
                        else:
                            pe.wait_ge(out_used, f.at(8, 6))
                    for q in range(2):
                        n = 2 * gr + q
                        for t in range(CC):
                            if gr == 0 and q == 0:
                                pe.wait_ge(ss_used, f.at(4, 3 + t))
                            z_hi = z2t[:, gr % 2, HI, q, t * P:(t + 1) * P]
                            z_lo = z2t[:, gr % 2, LO, q, t * P:(t + 1) * P]
                            ranks = ps[:, PAIR[t], :]
                            logits = ps[:, GATE_BANK, t * 2 * E_N:(t + 1) * 2 * E_N]
                            first, final = n == 0, n == NT - 1
                            nc.tensor.matmul(ranks, z_hi, wa[:, HI, n, :], start=first, stop=False)
                            nc.tensor.matmul(ranks, z_hi, wa[:, LO, n, :], start=False, stop=False)
                            nc.tensor.matmul(logits, z_hi, wg[:, n, :], start=first and t == 0, stop=False,
                                             skip_group_check=True)
                            nc.tensor.matmul(ranks, z_lo, wa[:, HI, n, :], start=False, stop=final)
                            last = nc.tensor.matmul(logits, z_lo, wg[:, n, :], start=False, stop=final,
                                                    skip_group_check=True)
                    last.then_inc(ha_ready if gr == GROUPS - 1 else zt_used, 1)

                if a:
                    pe.wait_ge(k_copied, a.at(16, 16))
                    pe.wait_ge(ct_done, a.at(8, 8))
                    pe.wait_ge(kt_done, a.at(16, 16))
                    for n in range(NT):
                        for c in range(CC):
                            last = mac3(ps[:, KC_BANK[c], :], ct[:, HI, n, c * P:(c + 1) * P],
                                        ct[:, LO, n, c * P:(c + 1) * P], kt[:, HI, n, :], kt[:, LO, n, :],
                                        n == 0, n == NT - 1)
                            if n == NT - 1:
                                last.then_inc(kc_ready, 1)

                if f:
                    for t in range(CC):
                        pe.wait_ge(hw_done, f.at(2, t + 1))
                        for j in range(HC):
                            last = nc.tensor.transpose(tp[:, t, j * P:(j + 1) * P], hw[:, t, j * P:(j + 1) * P],
                                                       ident[:, :])
                        last.then_inc(ht_ready, 1)
                for s in range(NT + Q_LAG):
                    if a and s < NT:
                        if s == 0:
                            if not f:
                                pe.wait_ge(w_lo, 4)
                            pe.wait_ge(z1_split, a.at(2, 2))
                        elif s == 1 and f:
                            pe.wait_ge(gate_read, f.at(1, 1))
                        elif s == 2:
                            pe.wait_ge(kc_split, a.at(2, 1))
                        elif s >= 3:
                            pe.wait_ge(q_exp, a.at(16, s - 2))
                        for c in range(CC):
                            last = mac3(ps[:, Q_RING[s % 3], :], opnd[:, HI, c, s * P:(s + 1) * P],
                                        opnd[:, LO, c, s * P:(s + 1) * P], wq[:, HI, c, :], wq[:, LO, c, :],
                                        c == 0, c == CC - 1)
                        last.then_inc(q_ready, 1)
                    if a and 1 <= s <= NT:
                        i = s - 1
                        pe.wait_ge(q_max, a.at(16, i + 1))
                        nc.tensor.matmul(ps[:, Q_RING[i % 3], :].rearrange("p (h d) -> p h d", h=HEADS), minus1[:, :],
                                         qmx[:, i % 4, :].unsqueeze(2).to_broadcast([P, HEADS, DH]),
                                         start=False, stop=True, skip_group_check=True).then_inc(q_sub, 1)
                    if a and s == CX_AT:
                        pe.wait_ge(kc_split, a.at(2, 2))
                        for j in range(HC):
                            two = slice(j * P, (j + 1) * P)
                            for c in range(CC):
                                last = mac3(ps[:, M_BANK, two], wv[:, HI, c, two], wv[:, LO, c, two],
                                            kc[:, HI, c, two], kc[:, LO, c, two], c == 0, c == CC - 1)
                        last.then_inc(cx_ready, 1)
                    if a and s in MM_AT:
                        half = MM_AT.index(s)
                        if half:
                            pe.wait_ge(m_read, a.at(4, 2))
                        else:
                            pe.wait_ge(bd_split, a.at(1, 1))
                        for j in (2 * half, 2 * half + 1):
                            two = slice(j * P, (j + 1) * P)
                            last = mac3(ps[:, M_BANK, (j % 2) * DIM:(j % 2 + 1) * DIM],
                                        bd[:, HI, two], bd[:, LO, two], wo[:, HI, j, :], wo[:, LO, j, :], True, True)
                        last.then_inc(m_ready, 1)
                    if a and s >= Q_LAG:
                        i = s - Q_LAG
                        pe.wait_ge(q_nrm, a.at(16, i + 1))
                        if i >= 2:
                            pe.wait_ge(qt_done, a.at(16, i - 1))
                        elif f:
                            pe.wait_ge(ht_done, f.at(2, i + 1))
                        for j in range(HC):
                            last = nc.tensor.transpose(tp[:, i % 2, j * P:(j + 1) * P],
                                                       ke[:, i % 8, j * P:(j + 1) * P], ident[:, :])
                        last.then_inc(qt_ready, 1)
                    if f and Y_AT <= s < Y_AT + 16:
                        u, half = (s - Y_AT) // 2, (s - Y_AT) % 2
                        t, nb = u // NB, u % NB
                        if half == 0:
                            if nb == 0:
                                pe.wait_ge(ht_done, f.at(2, t + 1))
                            if u >= 2:
                                pe.wait_ge(fin_done, f.at(8, u - 1))
                        for j in (2 * half, 2 * half + 1):
                            last = mac3(ps[:, PAIR[u % 2], :], hwt[:, HI, j, t * P:(t + 1) * P],
                                        hwt[:, LO, j, t * P:(t + 1) * P], wb[:, HI, j, nb * 512:nb * 512 + 512],
                                        wb[:, LO, j, nb * 512:nb * 512 + 512], j == 0, j == HC - 1)
                        if half:
                            last.then_inc(y_ready, 1)

                if not f:
                    pe.wait_ge(w_lo, W_PARTS)

                for i in range(8 if a else 0):
                    nb, o = i // CC, i % CC
                    if i == 0:
                        pe.wait_ge(qt_done, a.at(16, 16))
                        pe.wait_ge(m_split, a.at(1, 1))
                    if i == 0:
                        pe.wait_ge(m_read, a.at(4, 4))
                    elif i < 4:
                        pe.wait_ge(q_exp, a.at(16, 13 + i))
                    else:
                        pe.wait_ge(out_used, a.at(8, i - 3))
                    for j in range(HC):
                        last = mac3(ps[:, RING[i % 4], :], mm[:, HI, j, o * P:(o + 1) * P], mm[:, LO, j, o * P:(o + 1) * P],
                                    qn[:, HI, j, nb * 512:nb * 512 + 512], qn[:, LO, j, nb * 512:nb * 512 + 512],
                                    j == 0, j == HC - 1)
                    last.then_inc(out_ready, 1)
                    if o == 1 and nb:
                        if nb == 3:
                            pe.wait_ge(ss_used, a.at(4, 1))
                        elif f:
                            pe.wait_ge(fin_done, f.at(8, 6 + nb))
                        norms(a, nb - 1)

            turns(pe, body)


CX_AT, BD_AT, MM_AT, M_AT, Y_AT = 2, 4, (5, 7), 9, 1


def kt_bank(kg):
    return (kg + KT_LAG) % 2 if kg < 9 else 0


def kernel(x, ctx_4096, L0_xattn_Wq, L0_xattn_Wk, L0_xattn_Wv, L0_xattn_Wo, L0_xattn_bo, L0_xattn_g,
           L0_ffn_gate_w, L0_ffn_lora_A, L0_ffn_lora_B):
    import numpy as np
    import concourse.bacc as bacc
    from concourse import mybir as mb
    from concourse.bass_utils import run_bass_kernel_spmd

    def chunks(w):
        k, m = w.shape
        return np.ascontiguousarray(w.reshape(k // P, P, m).transpose(1, 0, 2).reshape(P, -1))

    arr = {k: np.asarray(v) for k, v in dict(
        x=x, ctx=ctx_4096, wq=L0_xattn_Wq, wk=L0_xattn_Wk, wv=L0_xattn_Wv, wo=L0_xattn_Wo, bo=L0_xattn_bo,
        g=L0_xattn_g, gate=L0_ffn_gate_w, la=L0_ffn_lora_A, lb=L0_ffn_lora_B).items()}
    n = arr["x"].shape[2]
    ins = {
        "x": np.ascontiguousarray(arr["x"]),
        "ctx": np.ascontiguousarray(arr["ctx"]),
        "wqT": chunks(arr["wq"].T), "wkT": chunks(arr["wk"].T), "wvT": chunks(arr["wv"].T),
        "woT": chunks(arr["wo"].T),
        "bo": np.ascontiguousarray(arr["bo"].reshape(-1, P).T),
        "g": np.ascontiguousarray(arr["g"].reshape(-1, P).T),
        "gateT": chunks(arr["gate"].T).reshape(P, n // P, E_N),
        "aT": chunks(arr["la"].reshape(-1, n).T),
        "bT": chunks(arr["lb"].transpose(0, 2, 1).reshape(-1, n)),
    }
    nc = bacc.Bacc("TRN2", target_bir_lowering=False, num_devices=1, dynamic_dma_scratch_size=1024)
    args = [nc.dram_tensor(f"in_{k}", a.shape, mb.dt.from_np(a.dtype), kind="ExternalInput").ap() for k, a in ins.items()]
    out = nc.dram_tensor("out_0", arr["x"].shape, mb.dt.float32, kind="ExternalOutput").ap()
    build(nc, *args, out)
    r = run_bass_kernel_spmd(nc, [{f"in_{k}": a for k, a in ins.items()}], core_ids=[0])
    return r.results[0]["out_0"]
```

```python
from contextlib import ExitStack

import concourse.bass as bass
from concourse import mybir

F32, F16, U32 = mybir.dt.float32, mybir.dt.float16, mybir.dt.uint32
ALU = mybir.AluOpType
ACT = mybir.ActivationFunctionType
X = mybir.AxisListType.X

P = 128
HI, LO = 0, 1
HEADS, DH, E_N = 8, 64, 8

S_Z = 2.0**8
S_W = 2.0**6
S_C = 2.0**4
S_K = 2.0**12
S_M = 2.0**8
S_Q = 2.0**10
S_H = 2.0**5

LN_EPS = 1e-5
NORM_FLOOR = 1e-12

RING = [5, 0, 4, 3]
Q_RING = [3, 0, 4]
PAIR = [1, 2]
GATE_BANK = RING[1]
KC_BANK = [4, 5]
M_BANK = 5
KT_LAG = 7
MERGE_AT = 11
KT_AT = [[4], [5], [6], [7, 8], [9, 10], [11, 12], [13, 14], [15]]
Q_LAG = 4
CX_AT, BD_AT, MM_AT, M_AT, Y_AT = 2, 4, (5, 7), 9, 1
SPLIT_AT = (17, 18)


class Turn:

    def __init__(self, reg, off):
        self.reg, self.off = reg, off

    def at(self, per, k):
        const = self.off * per + k
        return const if self.reg is None else self.reg * per + const

    @property
    def index(self):
        return self.off if self.reg is None else self.reg + self.off

    @property
    def next(self):
        return Turn(self.reg, self.off + 1)


def build(nc, x, ctx, wqT, wkT, wvT, woT, bo, g, gateT, aT, bT, out):
    B, DIM, N = x.shape
    HID = HEADS * DH
    CC = DIM // P
    HC = HID // P
    NB = N // 512
    NT = N // P
    KTILES = HC * NB
    GROUPS = NT // 2
    assert (B, DIM, N, HID) == (16, 256, 2048, 512)

    x_v = x.rearrange("b (c p) n -> b p c n", p=P)
    c_v = ctx.rearrange("b (c p) n -> b p c n", p=P)
    o_v = out.rearrange("b (c p) n -> b p c n", p=P)

    es = ExitStack()
    with es:
        def sb(name, shape, dt):
            return es.enter_context(nc.sbuf_tensor(name, shape, dt))

        def sem(name):
            return es.enter_context(nc.semaphore(name))

        wq = sb("wq", [P, 2, CC, HID], F16)
        wk = sb("wk", [P, 2, CC, HID], F16)
        wv = sb("wv", [P, 2, CC, HID], F16)
        wo = sb("wo", [P, 2, HC, DIM], F16)
        wa = sb("wa", [P, 2, NT, HID], F16)
        wb = sb("wb", [P, 2, HC, N], F16)
        wg = sb("wg", [P, NT, 2 * E_N], F16)
        wg_raw = sb("wg_raw", [P, NT, E_N], F32)
        ones = sb("ones", [P, 1], F32)
        ident = sb("ident", [P, P], F32)
        ident16 = sb("ident16", [P, P], F16)
        pairmask = sb("pairmask", [P, P], F32)
        experts = sb("experts", [P, E_N], F32)
        minus_half = sb("minus_half", [P, 4], F32)
        bo_c = sb("bo_c", [P, CC], F32)
        g_c = sb("g_c", [P, CC], F32)

        stage = sb("stage", [P, CC, N], F32)
        xres = sb("xres", [P, CC, N], F32)
        opnd = sb("opnd", [P, 2, CC, N], F16)
        ct_m = sb("ct_m", [P, 2 * NT * DIM], F16)
        yz = sb("yz", [P, CC, N], F32)
        zt = sb("zt", [P, 2 * 2 * 512], F16)
        kq = sb("kq", [P, 2, NT * HID], F16)
        ke = sb("ke", [P, 8, 512], F32)
        ssq = sb("ssq", [P, NB, 4], F32)
        rno = sb("rno", [P, NB, 4], F32)
        kmx = sb("kmx", [P, HC, NB], F32)
        nkm = sb("nkm", [P, HC], F32)
        ksum = sb("ksum", [P, HC], F32)
        krcp = sb("krcp", [P, HC], F32)
        nqm = sb("nqm", [P, 4, HEADS], F32)
        qsum = sb("qsum", [P, 4, HEADS], F32)
        qrcp = sb("qrcp", [P, 4, HEADS], F32)
        st1 = sb("st1", [P, CC, NB, 6], F32)
        st2 = sb("st2", [P, CC, NB, 6], F32)
        mv1 = sb("mv1", [P, CC, 2], F32)
        mv2 = sb("mv2", [P, CC, 2], F32)
        ve1 = sb("ve1", [P, CC], F32)
        ve2 = sb("ve2", [P, CC], F32)
        rs1 = sb("rs1", [P, CC], F32)
        rs2 = sb("rs2", [P, CC], F32)
        lgp = sb("lgp", [P, CC, 2 * E_N], F32)
        lg = sb("lg", [P, CC, E_N], F32)
        top = sb("top", [P, CC, 8], F32)
        who = sb("who", [P, CC, 8], U32)
        whof = sb("whof", [P, CC, 8], F32)
        gd = sb("gd", [P, CC], F32)
        ge = sb("ge", [P, CC], F32)
        gs = sb("gs", [P, CC], F32)
        gw = sb("gw", [P, 2, CC], F32)
        gpick = sb("gpick", [P, CC, 2, E_N], F32)
        carrier = sb("carrier", [P, 1], F32)
        gfull = sb("gfull", [P, CC, E_N], F32)

        kt = kq[:, :, :].rearrange("p h (n d) -> p h n d", d=HID)
        qn = kq[:, :, :].rearrange("p h (j n) -> p h j n", n=N)
        kraw = ke[:, :, :].rearrange("p (s t) n -> p s (t n)", s=2)
        sq = ke[:, :, :].rearrange("p (b o) n -> p b o n", o=2)
        ct = ct_m[:, :].rearrange("p (h n c) -> p h n c", h=2, n=NT)
        kc = ct_m[:, 0:2048].rearrange("p (h c d) -> p h c d", h=2, c=CC)
        bd = ct_m[:, 2048:3072].rearrange("p (h d) -> p h d", h=2)
        mm = ct_m[:, 3072:5120].rearrange("p (h j o) -> p h j o", h=2, j=HC)
        bdf = ct_m[:, 5120:6144].bitcast(F32)
        mf = ct_m[:, 6144:8192].bitcast(F32).rearrange("p (j o) -> p j o", j=HC)
        z2t = zt[:, :].rearrange("p (s h n t) -> p s h n t", s=2, h=2, n=2)
        hwt = zt[:, :].rearrange("p (h j t) -> p h j t", h=2, j=HC)
        hw = yz[:, 0, 0:CC * HID].rearrange("p (t d) -> p t d", t=CC)

        raw_w = wa[:, HI, :, :].rearrange("p n d -> p (n d)").bitcast(F32).rearrange("p (w n) -> p w n", w=4)
        raw_a = wb[:, :, :, :].rearrange("p h j n -> p (h j n)").bitcast(F32)
        raw_b = [yz[:, :, :].rearrange("p c n -> p (c n)"), xres[:, :, :].rearrange("p c n -> p (c n)")]

        ps = es.enter_context(nc.psum_tensor("ps", [P, 6, 512], F32))
        tp = es.enter_context(nc.psum_tensor("tp", [P, 2, 512], F32))

        def k_bank(i):
            return ps[:, RING[i % 4] if i < MERGE_AT else [RING[3], RING[0], RING[2]][(i - MERGE_AT) % 3], :]

        def kt_bank(f, kg):
            if not f:
                return [tp[:, 1, :], ps[:, PAIR[0], :], ps[:, PAIR[1], :]][kg % 3]
            if kg < 4:
                return [tp[:, 1, :], ps[:, PAIR[0], :], ps[:, PAIR[1], :], ps[:, GATE_BANK, :]][kg]
            return ps[:, RING[3], :] if kg in (12, 14) else tp[:, 0, :]

        w_in = [sem(f"w_in{i}") for i in range(4)]
        a_in, b_in, s_in = sem("a_in"), [sem("b_in0"), sem("b_in1")], sem("s_in")
        w_hi, w_lo = sem("w_hi"), sem("w_lo")
        consts, consts2, consts3 = sem("consts"), sem("consts2"), sem("consts3")
        ctx_in = [sem("ctx_in0"), sem("ctx_in1")]
        x_in = [sem("x_in0"), sem("x_in1")]
        res_in = [sem("res_in0"), sem("res_in1")]
        out_done = [[sem(f"out_done{c}{h}") for h in range(2)] for c in range(CC)]
        first_in = [sem(f"first_in{nb}") for nb in range(NB - 1)]
        first_hi, first_split = sem("first_hi"), sem("first_split")
        ctx_hi, ctx_split = sem("ctx_hi"), sem("ctx_split")
        k_ready, k_copied = sem("k_ready"), sem("k_copied")
        k_max, k_exp = sem("k_max"), sem("k_exp")
        kmx_done = sem("kmx_done")
        ct_ready, ct_done = sem("ct_ready"), sem("ct_done")
        kt_ready, kt_hi, kt_done = sem("kt_ready"), sem("kt_hi"), sem("kt_done")
        st1_done, mv1_done, rs1_done = sem("st1_done"), sem("mv1_done"), sem("rs1_done")
        z1_f, z1_hi, z1_split = sem("z1_f"), sem("z1_hi"), sem("z1_split")
        kc_ready, kc_hi, kc_split = sem("kc_ready"), sem("kc_hi"), sem("kc_split")
        cx_ready, bd_f, bd_hi, bd_split = sem("cx_ready"), sem("bd_f"), sem("bd_hi"), sem("bd_split")
        kr_done = sem("kr_done")
        m_ready, m_read, m_hi, m_split = sem("m_ready"), sem("m_read"), sem("m_hi"), sem("m_split")
        q_ready, q_max, q_neg, q_exp = sem("q_ready"), sem("q_max"), sem("q_neg"), sem("q_exp")
        q_sum, q_rcp, q_nrm = sem("q_sum"), sem("q_rcp"), sem("q_nrm")
        qt_ready, qt_hi, qt_done = sem("qt_ready"), sem("qt_hi"), sem("qt_done")
        out_ready, out_y, out_used = sem("out_ready"), sem("out_y"), sem("out_used")
        sqs_ready = sem("sqs_ready")
        ss_ready, ss_used, r_ready = sem("ss_ready"), sem("ss_used"), sem("r_ready")
        rb_ready, t_done = sem("rb_ready"), sem("t_done")
        x2_done = sem("x2_done")
        st2_done, mv2_done, rs2_done = sem("st2_done"), sem("mv2_done"), sem("rs2_done")
        z2_ready = sem("z2_ready")
        zt_ready, zt_hi, zt_done, zt_used = sem("zt_ready"), sem("zt_hi"), sem("zt_done"), sem("zt_used")
        ha_ready, gate_step, gate_exp = sem("ha_ready"), sem("gate_step"), sem("gate_exp")
        gate_read, hw_done = sem("gate_read"), sem("hw_done")
        ht_ready, ht_hi, ht_done = sem("ht_ready"), sem("ht_hi"), sem("ht_done")
        y_ready, fin_done = sem("y_ready"), sem("fin_done")
        G_STEPS = 15

        block = es.enter_context(nc.Block())

        def turns(eng, body):
            body(Turn(None, 0), None, True)
            with eng.Fori(0, B - 2) as i:
                body(Turn(i, 1), Turn(i, 0), True)
            body(Turn(None, B - 1), Turn(None, B - 2), False)
            body(None, Turn(None, B - 1), False)

        WEIGHTS = [(raw_w[:, i, :], w_in[i], w) for i, w in enumerate((
            wk[:, :, :, :].rearrange("p h c n -> p h (c n)"), wq[:, :, :, :].rearrange("p h c n -> p h (c n)"),
            wv[:, :, :, :].rearrange("p h c n -> p h (c n)"), wo[:, :, :, :].rearrange("p h c n -> p h (c n)")))]
        wa_f = wa[:, :, :, :].rearrange("p h c n -> p h (c n)")
        wb_f = wb[:, :, :, :].rearrange("p h c n -> p h (c n)")
        WEIGHTS.append((wg_raw[:, :, :], s_in, wg[:, :, :].rearrange("p c (h e) -> p h c e", h=2)))
        for i in range(4):
            WEIGHTS.append((raw_a[:, i * 2048:(i + 1) * 2048], a_in, wa_f[:, :, i * 2048:(i + 1) * 2048]))
        for i in range(4):
            WEIGHTS.append((raw_b[i // 2][:, (i % 2) * 2048:(i % 2 + 1) * 2048], b_in[i // 2],
                            wb_f[:, :, i * 2048:(i + 1) * 2048]))
        W_PARTS, A_PART, B_PARTS = len(WEIGHTS), 5, 4
        assert W_PARTS - B_PARTS == GROUPS + 1

        @block.sync
        def _(sp):
            def load_x(a):
                for c in range(CC):
                    sp.wait_ge(ctx_split, a.at(2, c + 1))
                    sp.dma_start(stage[:, c, :], x_v[a.index, :, c, :]).then_inc(x_in[c], 16)

            for nb in range(NB):
                cols = slice(nb * 512, nb * 512 + 512)
                if nb < NB - 1:
                    sp.dma_start(stage[:, :, cols], c_v[0, :, :, cols]).then_inc(first_in[nb], 16)
                else:
                    for c in range(CC):
                        sp.dma_start(stage[:, c, cols], c_v[0, :, c, cols]).then_inc(ctx_in[c], 16)
                if nb == 0:
                    sp.dma_start(raw_w[:, 0, :], wkT).then_inc(w_in[0], 16)
            for i, w in ((1, wqT), (2, wvT), (3, woT)):
                sp.dma_start(raw_w[:, i, :], w).then_inc(w_in[i], 16)
            for dst, src in ((wg_raw[:, :, :], gateT), (bo_c[:, :], bo), (g_c[:, :], g)):
                sp.dma_start(dst, src).then_inc(s_in, 16)
            load_x(Turn(None, 0))
            sp.dma_start(raw_a, aT).then_inc(a_in, 16)
            for i in range(2):
                sp.dma_start(raw_b[i], bT[:, i * 4096:(i + 1) * 4096]).then_inc(b_in[i], 16)

            def body(a, f, more):
                if more:
                    for c in range(CC):
                        sp.wait_ge(z1_split, a.at(2, c + 1))
                        sp.dma_start(stage[:, c, :], c_v[a.next.index, :, c, :]).then_inc(ctx_in[c], 16)
                for c in range(CC):
                    for h in range(2):
                        cols = slice(h * (N // 2), (h + 1) * (N // 2))
                        if f:
                            sp.wait_ge(fin_done, f.at(8, 4 * c + 2 * h + 2))
                            sp.dma_start(o_v[f.index, :, c, cols], xres[:, c, cols]).then_inc(out_done[c][h], 16)
                for c in range(CC):
                    for h in range(2):
                        cols = slice(h * (N // 2), (h + 1) * (N // 2))
                        if f:
                            sp.wait_ge(out_done[c][h], f.at(16, 16))
                        elif c + h == 0:
                            sp.wait_ge(w_lo, W_PARTS)
                        if a:
                            sp.dma_start(xres[:, c, cols], x_v[a.index, :, c, cols]).then_inc(res_in[h], 16)
                if more:
                    load_x(a.next)

            turns(sp, body)

        @block.gpsimd
        def _(pool):
            nc.gpsimd.memset(ident[:, :], 0.0).then_inc(consts, 1)
            nc.gpsimd.memset(ones[:, :], 1.0).then_inc(consts, 1)
            nc.gpsimd.memset(minus_half[:, :], -0.5).then_inc(consts, 1)
            for e in range(E_N):
                nc.gpsimd.memset(experts[:, e:e + 1], float(e)).then_inc(consts, 1)
            pool.wait_ge(consts, 11)
            nc.gpsimd.affine_select(out=ident[:, :], in_=ident[:, :], compare_op=ALU.not_equal, fill=1.0,
                                    base=0, pattern=[[-1, P]], channel_multiplier=1).then_inc(consts, 1)

            def body(a, f, more):
                if f:
                    add_x(f, 1)
                    inverse_norm(f, 3)
                    pool.wait_ge(res_in[1], f.at(32, 32))
                    add_x(f, 2)
                    add_x(f, 3)
                    rstd(f, ve2, rs2, mv2_done, rs2_done)
                if a:
                    rstd(a, ve1, rs1, mv1_done, rs1_done)
                    for i in range(NT):
                        pool.wait_ge(q_rcp, a.at(16, i + 1))
                        e = ke[:, i % 8, :].rearrange("p (h d) -> p h d", h=HEADS)
                        r = qrcp[:, i % 4, :].unsqueeze(2).to_broadcast([P, HEADS, DH])
                        nc.gpsimd.tensor_tensor(e, e, r, ALU.mult).then_inc(q_nrm, 1)
                    inverse_norm(a, 0)
                    inverse_norm(a, 1)
                    pool.wait_ge(res_in[0], a.at(32, 32))
                    add_x(a, 0)
                    inverse_norm(a, 2)

            def rstd(t, ve, rs, mv_done, rs_done):
                pool.wait_ge(mv_done, t.at(3, 3))
                nc.gpsimd.tensor_tensor(rs[:, :], ve[:, :], minus_half[:, 0:CC], ALU.pow).then_inc(rs_done, 1)

            def inverse_norm(t, nb):
                pool.wait_ge(ss_used, t.at(4, nb + 1))
                nc.gpsimd.tensor_tensor(rno[:, nb, :], ssq[:, nb, :], minus_half[:, :], ALU.pow).then_inc(r_ready, 1)

            def add_x(t, nb):
                pool.wait_ge(t_done, t.at(8, 2 * nb + 2))
                cols = slice(nb * 512, nb * 512 + 512)
                nc.gpsimd.tensor_tensor(xres[:, :, cols], xres[:, :, cols], yz[:, :, cols],
                                        ALU.add).then_inc(x2_done, 1)

            turns(pool, body)

        @block.scalar
        def _(act):
            def split_ctx(a, c):
                act.wait_ge(ctx_in[c], a.at(16, 16))
                nc.scalar.activation(opnd[:, HI, c, :], stage[:, c, :], ACT.Copy, scale=S_C).then_inc(ctx_hi, 1)

            def split_weight(i):
                raw, landed, parts = WEIGHTS[i]
                act.wait_ge(landed, 48 if landed is s_in else 16)
                if i == A_PART:
                    act.wait_ge(w_lo, A_PART - 1)
                if i >= W_PARTS - B_PARTS:
                    act.wait_ge(w_lo, W_PARTS - B_PARTS)
                nc.scalar.activation(parts[:, HI, :], raw, ACT.Copy, scale=S_W).then_inc(w_hi, 1)

            for nb in range(NB):
                cols = slice(nb * 512, nb * 512 + 512)
                if nb < NB - 1:
                    act.wait_ge(first_in[nb], 16)
                    nc.scalar.activation(opnd[:, HI, :, cols], stage[:, :, cols], ACT.Copy,
                                         scale=S_C).then_inc(first_hi, 1)
                else:
                    for c in range(CC):
                        act.wait_ge(ctx_in[c], 16)
                        nc.scalar.activation(opnd[:, HI, c, cols], stage[:, c, cols], ACT.Copy,
                                             scale=S_C).then_inc(ctx_hi, 1)
                if nb == 0:
                    split_weight(0)

            def exp_k(a, j):
                act.wait_ge(k_max, a.at(4, j + 1))
                nc.scalar.activation(kraw[:, j % 2, :], kraw[:, j % 2, :], ACT.Exp, bias=nkm[:, j:j + 1],
                                     accum_out=ksum[:, j:j + 1]).then_inc(k_exp, 1)

            def kt_high(a, f, kg):
                act.wait_ge(kt_ready, a.at(16, kg + 1))
                j, t = kg // 4, kg % 4
                src = kt_bank(f, kg).rearrange("p (n d) -> p n d", n=4)
                nc.scalar.activation(kt[:, HI, 4 * t:4 * t + 4, j * P:(j + 1) * P], src, ACT.Copy,
                                     scale=S_K).then_inc(kt_hi, 1)

            def k_copy(a, i):
                act.wait_ge(k_ready, a.at(16, i + 1))
                nc.scalar.activation(ke[:, i % 8, :], k_bank(i), ACT.Copy, scale=1.0 / (S_C * S_W)).then_inc(k_copied, 1)

            def ct_copy(a, m):
                act.wait_ge(ct_ready, a.at(8, m + 1))
                src = tp[:, 0, :].bitcast(F16).rearrange("p (h n c) -> p h n c", h=2, n=2)
                nc.scalar.activation(ct[:, :, 2 * m:2 * m + 2, :], src, ACT.Copy).then_inc(ct_done, 1)

            def z2_high(f, gr):
                act.wait_ge(zt_ready, f.at(8, gr + 1))
                if gr >= 2:
                    act.wait_ge(zt_used, f.at(GROUPS - 1, gr - 1))
                nc.scalar.activation(z2t[:, gr % 2, HI, :, :], tp[:, 1, :].rearrange("p (n t) -> p n t", n=2),
                                     ACT.Copy, scale=S_Z).then_inc(zt_hi, 1)

            def out_tile(a, i):
                nb, o = i // CC, i % CC
                if i == 0 and a.reg is None and a.off == 0:
                    act.wait_ge(w_lo, W_PARTS)
                act.wait_ge(out_ready, a.at(8, i + 1))
                tile = ps[:, RING[i % 4], :]
                nc.scalar.activation(yz[:, o, nb * 512:nb * 512 + 512], tile, ACT.Identity,
                                     bias=bo_c[:, o:o + 1], scale=DH**-0.5 / (S_M * S_Q)).then_inc(out_y, 1)
                nc.scalar.activation(sq[:, nb, o, :], tile, ACT.Square,
                                     bias=bo_c[:, o:o + 1], scale=DH**-0.5 / (S_M * S_Q)).then_inc(out_used, 1)

            def body(a, f, more):
                for i in range(MERGE_AT if a else 0):
                    k_copy(a, i)
                    if i % 2:
                        ct_copy(a, i // 2)
                    if i == 5:
                        exp_k(a, 0)
                    if f and i == MERGE_AT - 1:
                        z2_high(f, 0)
                    if i >= KT_LAG:
                        kt_high(a, f, i - KT_LAG)
                    if i == MERGE_AT - 1:
                        exp_k(a, 1)
                if not a:
                    z2_high(f, 0)
                for u in range(GROUPS):
                    i = MERGE_AT + u
                    if a and i < KTILES:
                        k_copy(a, i)
                        if i % 2:
                            ct_copy(a, i // 2)
                        if i == 13:
                            exp_k(a, 2)
                    elif a and i == KTILES:
                        exp_k(a, 3)
                    if f and u + 1 < GROUPS:
                        z2_high(f, u + 1)
                    for kg in KT_AT[u] if a else []:
                        kt_high(a, f, kg)
                    if not f:
                        split_weight(u + 1)
                if a:
                    act.wait_ge(ct_ready, a.at(8, 8))
                    for c in range(CC):
                        act.wait_ge(z1_f, a.at(2, c + 1))
                        nc.scalar.activation(opnd[:, HI, c, :], stage[:, c, :], ACT.Copy, scale=S_Z).then_inc(z1_hi, 1)
                if not f:
                    for i in range(W_PARTS - B_PARTS, W_PARTS):
                        split_weight(i)
                if f:
                    act.wait_ge(gate_step, f.at(G_STEPS, G_DIFF))
                    nc.scalar.activation(ge[:, :], gd[:, :], ACT.Exp).then_inc(gate_exp, 1)
                if a:
                    for c in range(CC):
                        act.wait_ge(kc_ready, a.at(2, c + 1))
                        nc.scalar.activation(kc[:, HI, c, :], ps[:, KC_BANK[c], :], ACT.Copy,
                                             scale=1.0 / (S_K * S_C)).then_inc(kc_hi, 1)
                if f:
                    for t in range(CC):
                        act.wait_ge(ht_ready, f.at(2, t + 1))
                        nc.scalar.activation(hwt[:, HI, :, t * P:(t + 1) * P],
                                             tp[:, t, :].rearrange("p (j n) -> p j n", j=HC), ACT.Copy).then_inc(ht_hi, 1)
                for s in range(1, NT + Q_LAG if a else 0):
                    if s <= NT:
                        act.wait_ge(q_neg, a.at(16, s))
                        for h in range(HEADS):
                            cols = slice(h * DH, (h + 1) * DH)
                            last = nc.scalar.activation(ke[:, (s - 1) % 8, cols], ps[:, Q_RING[(s - 1) % 3], cols], ACT.Exp,
                                                        bias=nqm[:, (s - 1) % 4, h:h + 1], scale=1.0 / (S_Z * S_W))
                        last.then_inc(q_exp, 1)
                    if s == BD_AT:
                        act.wait_ge(bd_f, a.at(1, 1))
                        nc.scalar.activation(bd[:, HI, :], bdf, ACT.Copy).then_inc(bd_hi, 1)
                    if s == M_AT:
                        act.wait_ge(m_read, a.at(4, 4))
                        nc.scalar.activation(mm[:, HI, :, :], mf, ACT.Copy).then_inc(m_hi, 1)
                    if s >= Q_LAG:
                        i = s - Q_LAG
                        act.wait_ge(qt_ready, a.at(16, i + 1))
                        nc.scalar.activation(qn[:, HI, :, i * P:(i + 1) * P],
                                             tp[:, i % 2, :].rearrange("p (j n) -> p j n", j=HC),
                                             ACT.Copy, scale=S_Q).then_inc(qt_hi, 1)
                    if s > NT:
                        out_tile(a, s - NT - 1)
                    if more and s in SPLIT_AT:
                        act.wait_ge(q_ready, a.at(16, 16))
                        split_ctx(a.next, SPLIT_AT.index(s))
                for i in range(Q_LAG - 1, 8 if a else 0):
                    out_tile(a, i)

            G_DIFF = 7
            turns(act, body)

        @block.vector
        def _(dve):
            def low(out_, raw, scale, high):
                return nc.vector.scalar_tensor_tensor(out=out_, in0=raw, scalar=scale, in1=high,
                                                      op0=ALU.mult, op1=ALU.subtract)

            def split_ctx(a, c):
                dve.wait_ge(ctx_hi, a.at(2, c + 1))
                low(opnd[:, LO, c, :], stage[:, c, :], S_C, opnd[:, HI, c, :]).then_inc(ctx_split, 1)

            def split_weight(i):
                raw, _, parts = WEIGHTS[i]
                dve.wait_ge(w_hi, i + 1)
                low(parts[:, LO, :], raw, S_W, parts[:, HI, :]).then_inc(w_lo, 1)

            nc.vector.memset(pairmask[:, :], 0.0).then_inc(consts3, 1)
            dve.wait_ge(consts3, 1)
            nc.vector.memset(pairmask[0:DH, 0:DH], 1.0).then_inc(consts3, 1)
            nc.vector.memset(pairmask[DH:P, DH:P], 1.0).then_inc(consts3, 1)
            dve.wait_ge(consts, 12)
            nc.vector.tensor_copy(ident16[:, :], ident[:, :]).then_inc(consts2, 1)
            dve.wait_ge(consts2, 1)
            dve.wait_ge(consts3, 3)
            for nb in range(NB):
                cols = slice(nb * 512, nb * 512 + 512)
                if nb < NB - 1:
                    dve.wait_ge(first_hi, nb + 1)
                    low(opnd[:, LO, :, cols], stage[:, :, cols], S_C, opnd[:, HI, :, cols]).then_inc(first_split, 1)
                else:
                    for c in range(CC):
                        dve.wait_ge(ctx_hi, c + 1)
                        low(opnd[:, LO, c, cols], stage[:, c, cols], S_C, opnd[:, HI, c, cols]).then_inc(ctx_split, 1)
                if nb == 0:
                    split_weight(0)

            def carry():
                nc.vector.memset(carrier[:, :], 0.0)

            def max_k(a, i):
                dve.wait_ge(k_copied, a.at(16, i + 1))
                nc.vector.reduce_max(kmx[:, i // 4, i % 4:i % 4 + 1], ke[:, i % 8, :], X).then_inc(kmx_done, 1)
                if i % 4 == 3:
                    dve.wait_ge(kmx_done, a.at(16, i + 1))
                    nc.vector.tensor_reduce(nkm[:, i // 4:i // 4 + 1], kmx[:, i // 4, :], X, ALU.max,
                                            negate=True).then_inc(k_max, 1)

            def kt_low(a, f, kg):
                dve.wait_ge(kt_hi, a.at(16, kg + 1))
                j, t = kg // 4, kg % 4
                src = kt_bank(f, kg).rearrange("p (n d) -> p n d", n=4)
                where = (slice(4 * t, 4 * t + 4), slice(j * P, (j + 1) * P))
                low(kt[:, LO, where[0], where[1]], src, S_K, kt[:, HI, where[0], where[1]]).then_inc(kt_done, 1)

            def sum_squares(t, nb):
                dve.wait_ge(out_used, t.at(8, 2 * nb + 2))
                nc.vector.tensor_tensor(sq[:, nb, 0, :], sq[:, nb, 0, :], sq[:, nb, 1, :], ALU.add).then_inc(sqs_ready, 1)

            def floor_norm(t, nb):
                dve.wait_ge(ss_ready, t.at(4, nb + 1))
                nc.vector.tensor_scalar(ssq[:, nb, :], ps[:, PAIR[nb % 2], 0:4], NORM_FLOOR**2, None,
                                        ALU.max).then_inc(ss_used, 1)

            def scale_y(t, nb):
                dve.wait_ge(rb_ready, t.at(4, nb + 1))
                for o in range(CC):
                    y = yz[:, o, nb * 512:nb * 512 + 512]
                    nc.vector.scalar_tensor_tensor(out=y, in0=y, scalar=g_c[:, o:o + 1], in1=ps[:, PAIR[nb % 2], :],
                                                   op0=ALU.mult, op1=ALU.mult).then_inc(t_done, 1)

            def stats2(f, nb):
                dve.wait_ge(x2_done, f.at(4, nb + 1))
                for o in range(CC):
                    nc.vector.bn_stats(st2[:, o, nb, :], xres[:, o, nb * 512:nb * 512 + 512]).then_inc(st2_done, 1)

            def mean_rstd(t, st_done, st, mv, ve, rs, mv_done, rs_done):
                dve.wait_ge(st_done, t.at(8, 8))
                carry()
                for o in range(CC):
                    nc.vector.bn_aggr(mv[:, o, :], st[:, o, :, :].rearrange("p b s -> p (b s)")).then_inc(mv_done, 1)
                dve.wait_ge(mv_done, t.at(3, 2))
                nc.vector.tensor_scalar(ve[:, :], mv[:, :, 1], LN_EPS, None, ALU.add).then_inc(mv_done, 1)
                dve.wait_ge(rs_done, t.at(1, 1))

            def z2_low(f, gr):
                dve.wait_ge(zt_hi, f.at(8, gr + 1))
                low(z2t[:, gr % 2, LO, :, :], tp[:, 1, :].rearrange("p (n t) -> p n t", n=2), S_Z,
                    z2t[:, gr % 2, HI, :, :]).then_inc(zt_done, 1)

            def z2_rows(f, o):
                nc.vector.tensor_scalar(yz[:, o, :], xres[:, o, :], mv2[:, o, 0:1], rs2[:, o:o + 1],
                                        ALU.subtract, ALU.mult).then_inc(z2_ready, 1)

            def gate(f):
                n = [0]

                def step(ins, wait=True):
                    n[0] += 1
                    ins.then_inc(gate_step, 1)
                    if wait:
                        dve.wait_ge(gate_step, f.at(G_STEPS, n[0]))

                dve.wait_ge(ha_ready, f.at(1, 1))
                nc.vector.tensor_scalar(lgp[:, :, :], ps[:, GATE_BANK, 0:CC * 2 * E_N].rearrange("p (t e) -> p t e", t=CC),
                                        1.0 / (S_Z * S_W), None, ALU.mult).then_inc(gate_read, 1)
                dve.wait_ge(gate_read, f.at(1, 1))
                step(nc.vector.tensor_tensor(lg[:, :, :], lgp[:, :, 0:E_N], lgp[:, :, E_N:2 * E_N], ALU.add))
                carry()
                step(nc.vector.max(top[:, 0, :], lg[:, 0, :]), False)
                step(nc.vector.max(top[:, 1, :], lg[:, 1, :]), False)
                dve.wait_ge(gate_step, f.at(G_STEPS, 3))
                carry()
                step(nc.vector.max_index(who[:, 0, :], top[:, 0, :], lg[:, 0, :]), False)
                step(nc.vector.max_index(who[:, 1, :], top[:, 1, :], lg[:, 1, :]))
                step(nc.vector.tensor_copy(whof[:, :, :], who[:, :, :]), False)
                step(nc.vector.tensor_tensor(gd[:, :], top[:, :, 1], top[:, :, 0], ALU.subtract))
                dve.wait_ge(gate_exp, f.at(1, 1))
                step(nc.vector.tensor_scalar(gs[:, :], ge[:, :], 1.0, None, ALU.add))
                step(nc.vector.reciprocal(gw[:, 0, :], gs[:, :]))
                step(nc.vector.tensor_tensor(gw[:, 1, :], ge[:, :], gw[:, 0, :], ALU.mult))
                for t in range(CC):
                    for r in range(2):
                        step(nc.vector.tensor_scalar(gpick[:, t, r, :], experts[:, :], whof[:, t, r:r + 1],
                                                     gw[:, r, t:t + 1], ALU.is_equal, ALU.mult), t + r == 2)
                step(nc.vector.tensor_tensor(gfull[:, :, :], gpick[:, :, 0, :], gpick[:, :, 1, :], ALU.add))
                assert n[0] == G_STEPS
                for t in range(CC):
                    nc.vector.scalar_tensor_tensor(
                        out=hw[:, t, :].rearrange("p (e r) -> p e r", e=E_N),
                        in0=ps[:, PAIR[t], :].rearrange("p (e r) -> p e r", e=E_N), scalar=S_H / (S_Z * S_W),
                        in1=gfull[:, t, :].unsqueeze(2).to_broadcast([P, E_N, DH]),
                        op0=ALU.mult, op1=ALU.mult).then_inc(hw_done, 1)

            def body(a, f, more):
                tail = {}
                if f:
                    tail = {0: [(scale_y, 2), (floor_norm, 3)], 1: [(stats2, 0), (stats2, 1)], 2: [(scale_y, 3)],
                            3: [(stats2, 2)], 4: [(stats2, 3)]}
                if f:
                    sum_squares(f, 3)
                for i in range(MERGE_AT):
                    if a:
                        max_k(a, i)
                        if f and i == MERGE_AT - 1:
                            z2_low(f, 0)
                        if i >= KT_LAG:
                            kt_low(a, f, i - KT_LAG)
                    for what, nb in tail.get(i, []):
                        what(f, nb)
                    if f and i == 5:
                        mean_rstd(f, st2_done, st2, mv2, ve2, rs2, mv2_done, rs2_done)
                    if f and i in (6, 7):
                        z2_rows(f, i - 6)
                if not a:
                    z2_low(f, 0)
                for u in range(GROUPS):
                    i = MERGE_AT + u
                    if a and i < KTILES:
                        max_k(a, i)
                    if f and u + 1 < GROUPS:
                        z2_low(f, u + 1)
                    for kg in KT_AT[u] if a else []:
                        kt_low(a, f, kg)
                    if not f:
                        split_weight(u + 1)
                    if a:
                        o, nb = u // NB, u % NB
                        if nb == 0:
                            dve.wait_ge(x_in[o], a.at(16, 16))
                        nc.vector.bn_stats(st1[:, o, nb, :], stage[:, o, nb * 512:nb * 512 + 512]).then_inc(st1_done, 1)
                if not f:
                    dve.wait_ge(s_in, 48)
                    nc.vector.tensor_scalar(g_c[:, :], g_c[:, :], DIM**0.5, None, ALU.mult).then_inc(consts2, 1)
                    dve.wait_ge(consts2, 2)
                if a:
                    mean_rstd(a, st1_done, st1, mv1, ve1, rs1, mv1_done, rs1_done)
                    for o in range(CC):
                        nc.vector.tensor_scalar(stage[:, o, :], stage[:, o, :], mv1[:, o, 0:1], rs1[:, o:o + 1],
                                                ALU.subtract, ALU.mult).then_inc(z1_f, 1)
                    for o in range(CC):
                        dve.wait_ge(z1_hi, a.at(2, o + 1))
                        low(opnd[:, LO, o, :], stage[:, o, :], S_Z, opnd[:, HI, o, :]).then_inc(z1_split, 1)
                    dve.wait_ge(k_exp, a.at(4, 4))
                    nc.vector.reciprocal(krcp[:, :], ksum[:, :]).then_inc(kr_done, 1)
                if f:
                    gate(f)
                else:
                    for i in range(W_PARTS - B_PARTS, W_PARTS):
                        split_weight(i)
                if a:
                    for c in range(CC):
                        dve.wait_ge(kc_hi, a.at(2, c + 1))
                        low(kc[:, LO, c, :], ps[:, KC_BANK[c], :], 1.0 / (S_K * S_C), kc[:, HI, c, :]).then_inc(kc_split, 1)
                if f:
                    for t in range(CC):
                        dve.wait_ge(ht_hi, f.at(2, t + 1))
                        low(hwt[:, LO, :, t * P:(t + 1) * P], tp[:, t, :].rearrange("p (j n) -> p j n", j=HC), 1.0,
                            hwt[:, HI, :, t * P:(t + 1) * P]).then_inc(ht_done, 1)
                for s in range(NT + Q_LAG + 1):
                    if a and s >= Q_LAG + 1:
                        i = s - Q_LAG - 1
                        dve.wait_ge(qt_hi, a.at(16, i + 1))
                        cols = slice(i * P, (i + 1) * P)
                        low(qn[:, LO, :, cols], tp[:, i % 2, :].rearrange("p (j n) -> p j n", j=HC), S_Q,
                            qn[:, HI, :, cols]).then_inc(qt_done, 1)
                    if a and s < NT:
                        dve.wait_ge(q_ready, a.at(16, s + 1))
                        nc.vector.tensor_reduce(nqm[:, s % 4, :],
                                                ps[:, Q_RING[s % 3], :].rearrange("p (h d) -> p h d", h=HEADS),
                                                X, ALU.max, negate=True).then_inc(q_max, 1)
                        dve.wait_ge(q_max, a.at(16, s + 1))
                        nc.vector.tensor_scalar(nqm[:, s % 4, :], nqm[:, s % 4, :], 1.0 / (S_Z * S_W), None,
                                                ALU.mult).then_inc(q_neg, 1)
                    if a and 1 <= s <= NT:
                        i = s - 1
                        dve.wait_ge(q_exp, a.at(16, i + 1))
                        if i >= 4:
                            dve.wait_ge(q_nrm, a.at(16, i - 3))
                        nc.vector.reduce_sum(qsum[:, i % 4, :], ke[:, i % 8, :].rearrange("p (h d) -> p h d", h=HEADS),
                                             X).then_inc(q_sum, 1)
                        dve.wait_ge(q_sum, a.at(16, i + 1))
                        nc.vector.reciprocal(qrcp[:, i % 4, :], qsum[:, i % 4, :]).then_inc(q_rcp, 1)
                    if a and s == CX_AT + 1:
                        dve.wait_ge(cx_ready, a.at(1, 1))
                        nc.vector.scalar_tensor_tensor(
                            out=bdf.rearrange("p (j d) -> p j d", j=HC),
                            in0=ps[:, M_BANK, :].rearrange("p (j d) -> p j d", j=HC), scalar=1.0 / S_W,
                            in1=pairmask[:, :].unsqueeze(1).to_broadcast([P, HC, P]),
                            op0=ALU.mult, op1=ALU.mult).then_inc(bd_f, 1)
                    if a and s == BD_AT:
                        dve.wait_ge(bd_hi, a.at(1, 1))
                        nc.vector.tensor_tensor(bd[:, LO, :], bdf, bd[:, HI, :], ALU.subtract).then_inc(bd_split, 1)
                    if a and s in (MM_AT[0] + 1, MM_AT[1] + 1):
                        half = MM_AT.index(s - 1)
                        dve.wait_ge(kr_done, a.at(1, 1))
                        dve.wait_ge(m_ready, a.at(2, half + 1))
                        for j in (2 * half, 2 * half + 1):
                            nc.vector.tensor_scalar(mf[:, j, :], ps[:, M_BANK, (j % 2) * DIM:(j % 2 + 1) * DIM],
                                                    krcp[:, j:j + 1], S_M / S_W, ALU.mult, ALU.mult).then_inc(m_read, 1)
                    if a and s == M_AT:
                        dve.wait_ge(m_hi, a.at(1, 1))
                        nc.vector.tensor_tensor(mm[:, LO, :, :], mf, mm[:, HI, :, :], ALU.subtract).then_inc(m_split, 1)
                    if f and s >= Y_AT + 2 and (s - Y_AT) % 2 == 0 and s < Y_AT + 18:
                        u = (s - Y_AT) // 2 - 1
                        t, nb = u // NB, u % NB
                        dve.wait_ge(y_ready, f.at(8, u + 1))
                        acc = xres[:, t, nb * 512:nb * 512 + 512]
                        nc.vector.scalar_tensor_tensor(out=acc, in0=ps[:, PAIR[u % 2], :], scalar=1.0 / (S_H * S_W),
                                                       in1=acc, op0=ALU.mult, op1=ALU.add).then_inc(fin_done, 1)
                    if a and s == NT + Q_LAG - 1:
                        sum_squares(a, 0)
                    if more and s - 1 in SPLIT_AT:
                        split_ctx(a.next, SPLIT_AT.index(s - 1))
                for nb in range(NB - 1 if a else 0):
                    if nb:
                        sum_squares(a, nb)
                        scale_y(a, nb - 1)
                    floor_norm(a, nb)

            turns(dve, body)

        @block.tensor
        def _(pe):
            def mac3(acc, l_hi, l_lo, r_hi, r_lo, first, last):
                nc.tensor.matmul(acc, l_hi, r_hi, start=first, stop=False)
                nc.tensor.matmul(acc, l_hi, r_lo, start=False, stop=False)
                return nc.tensor.matmul(acc, l_lo, r_hi, start=False, stop=last)

            pe.wait_ge(consts2, 1)

            def squared_norms(t, f, nb):
                pe.wait_ge(sqs_ready, t.at(4, nb + 1))
                if nb >= 2:
                    pe.wait_ge(t_done, t.at(8, 2 * nb - 2))
                elif f:
                    pe.wait_ge(fin_done, f.at(8, 7 + nb))
                for n in range(4):
                    last = nc.tensor.matmul(ps[:, PAIR[nb % 2], n:n + 1], sq[:, nb, 0, n * P:(n + 1) * P], ones[:, :],
                                            start=True, stop=True)
                last.then_inc(ss_ready, 1)

            def spread_norms(t, nb):
                pe.wait_ge(r_ready, t.at(4, nb + 1))
                for n in range(4):
                    last = nc.tensor.transpose(ps[:, PAIR[nb % 2], n * P:(n + 1) * P],
                                               rno[:, nb, n:n + 1].to_broadcast([P, P]), ident[:, :])
                last.then_inc(rb_ready, 1)

            def out_tile(a, f, i):
                nb, o = i // CC, i % CC
                if o == 0:
                    pe.wait_ge(qt_done, a.at(16, 4 * nb + 4))
                if i == 0:
                    pe.wait_ge(m_split, a.at(1, 1))
                elif i < 4:
                    pe.wait_ge(q_exp, a.at(16, 13 + i))
                else:
                    pe.wait_ge(out_used, a.at(8, i - 3))
                for j in range(HC):
                    last = mac3(ps[:, RING[i % 4], :], mm[:, HI, j, o * P:(o + 1) * P], mm[:, LO, j, o * P:(o + 1) * P],
                                qn[:, HI, j, nb * 512:nb * 512 + 512], qn[:, LO, j, nb * 512:nb * 512 + 512],
                                j == 0, j == HC - 1)
                last.then_inc(out_ready, 1)
                if i >= 3:
                    if o:
                        squared_norms(a, f, nb - 1)
                    else:
                        spread_norms(a, nb - 2)

            def k_tile(a, f, i):
                j, nb = i // NB, i % NB
                if not f and i == 0:
                    pe.wait_ge(w_lo, 1)
                if f and i == 0 or not f and i == NB - 1:
                    pe.wait_ge(ctx_split, a.at(2, 2))
                elif not f and i < NB - 1:
                    pe.wait_ge(first_split, i + 1)
                if i >= 4:
                    pe.wait_ge(k_copied, a.at(16, i - 3 if i < MERGE_AT + 2 else i - 2))
                elif f:
                    pe.wait_ge(out_used, f.at(8, 5 + i))
                for c in range(CC):
                    last = mac3(k_bank(i), wk[:, HI, c, j * P:(j + 1) * P], wk[:, LO, c, j * P:(j + 1) * P],
                                opnd[:, HI, c, nb * 512:nb * 512 + 512], opnd[:, LO, c, nb * 512:nb * 512 + 512],
                                c == 0, c == CC - 1)
                last.then_inc(k_ready, 1)

            def ct_blocks(a, f, m):
                if m:
                    pe.wait_ge(ct_done, a.at(8, m))
                if f and 2 * m > MERGE_AT:
                    pe.wait_ge(kt_done, a.at(16, KT_AT[2 * m - MERGE_AT][-1] + 1))
                dst = tp[:, 0, :].bitcast(F16).rearrange("p (h n c) -> p h n c", h=2, n=2)
                for h in range(2):
                    for q in range(2):
                        for c in range(CC):
                            n = 2 * m + q
                            last = nc.tensor.transpose(dst[:, h, q, c * P:(c + 1) * P],
                                                       opnd[:, h, c, n * P:(n + 1) * P], ident16[:, :])
                last.then_inc(ct_ready, 1)

            def kt_blocks(a, f, kg):
                j, t = kg // 4, kg % 4
                if t == 0:
                    pe.wait_ge(k_exp, a.at(4, j + 1))
                if not f:
                    if kg > 2:
                        pe.wait_ge(kt_done, a.at(16, kg - 2))
                elif kg in (1, 2):
                    pe.wait_ge(t_done, f.at(8, 4 + 2 * kg))
                elif kg in (3, 12):
                    pe.wait_ge(k_copied, a.at(16, 10 if kg == 3 else 15))
                elif kg > 12:
                    pe.wait_ge(kt_done, a.at(16, kg - 1))
                elif kg > 3:
                    m = min((kg + KT_LAG + 1) // 2, NT // 2) if kg < 8 else (7 if kg == 8 else 8)
                    pe.wait_ge(ct_done, a.at(8, m))
                    if kg > 4:
                        pe.wait_ge(kt_done, a.at(16, kg))
                for q in range(4):
                    n = 4 * t + q
                    last = nc.tensor.transpose(kt_bank(f, kg)[:, q * P:(q + 1) * P],
                                               kraw[:, j % 2, n * P:(n + 1) * P], ident[:, :])
                last.then_inc(kt_ready, 1)

            def z2_blocks(f, gr):
                for q in range(2):
                    for t in range(CC):
                        n = 2 * gr + q
                        last = nc.tensor.transpose(tp[:, 1, (q * CC + t) * P:(q * CC + t + 1) * P],
                                                   yz[:, t, n * P:(n + 1) * P], ident[:, :])
                last.then_inc(zt_ready, 1)

            def project(a, f, gr, q):
                if gr + q == 0:
                    if a:
                        pe.wait_ge(kt_done, a.at(16, 4))
                    else:
                        pe.wait_ge(out_used, f.at(8, 6))
                n = 2 * gr + q
                for t in range(CC):
                    if n == 0:
                        pe.wait_ge(t_done, f.at(8, 6 + 2 * t))
                    z_hi = z2t[:, gr % 2, HI, q, t * P:(t + 1) * P]
                    z_lo = z2t[:, gr % 2, LO, q, t * P:(t + 1) * P]
                    ranks = ps[:, PAIR[t], :]
                    logits = ps[:, GATE_BANK, t * 2 * E_N:(t + 1) * 2 * E_N]
                    first, final = n == 0, n == NT - 1
                    nc.tensor.matmul(ranks, z_hi, wa[:, HI, n, :], start=first, stop=False)
                    nc.tensor.matmul(ranks, z_hi, wa[:, LO, n, :], start=False, stop=False)
                    nc.tensor.matmul(logits, z_hi, wg[:, n, :], start=first and t == 0, stop=False,
                                     skip_group_check=True)
                    nc.tensor.matmul(ranks, z_lo, wa[:, HI, n, :], start=False, stop=final)
                    last = nc.tensor.matmul(logits, z_lo, wg[:, n, :], start=False, stop=final, skip_group_check=True)
                if q:
                    last.then_inc(ha_ready if gr == GROUPS - 1 else zt_used, 1)

            def body(a, f, more):
                for i in range(MERGE_AT if a else 0):
                    k_tile(a, f, i)
                    if f and i == 0:
                        spread_norms(f, 2)
                    if f and i == 1:
                        squared_norms(f, None, 3)
                    if f and i == 2:
                        spread_norms(f, 3)
                    if i % 2:
                        ct_blocks(a, f, i // 2)
                    if f and i == MERGE_AT - 1:
                        pe.wait_ge(kt_done, a.at(16, 1))
                        pe.wait_ge(z2_ready, f.at(2, 2))
                        z2_blocks(f, 0)
                    if i >= KT_LAG:
                        kt_blocks(a, f, i - KT_LAG)
                if f and not a:
                    spread_norms(f, 2)
                    squared_norms(f, None, 3)
                    spread_norms(f, 3)

                if f and not a:
                    pe.wait_ge(z2_ready, f.at(2, 2))
                    z2_blocks(f, 0)
                for u in range(GROUPS):
                    i = MERGE_AT + u
                    if a and i < KTILES:
                        k_tile(a, f, i)
                        if i % 2:
                            ct_blocks(a, f, i // 2)
                    if f:
                        pe.wait_ge(zt_done, f.at(8, u + 1))
                        if u + 1 < GROUPS:
                            z2_blocks(f, u + 1)
                        project(a, f, u, 0)
                    if a:
                        kt_blocks(a, f, KT_AT[u][0])
                    if f:
                        project(a, f, u, 1)
                    for kg in KT_AT[u][1:] if a else []:
                        kt_blocks(a, f, kg)

                if a:
                    pe.wait_ge(k_copied, a.at(16, 16))
                    pe.wait_ge(ct_done, a.at(8, 8))
                    pe.wait_ge(kt_done, a.at(16, 16))
                    for n in range(NT):
                        for c in range(CC):
                            last = mac3(ps[:, KC_BANK[c], :], ct[:, HI, n, c * P:(c + 1) * P],
                                        ct[:, LO, n, c * P:(c + 1) * P], kt[:, HI, n, :], kt[:, LO, n, :],
                                        n == 0, n == NT - 1)
                            if n == NT - 1:
                                last.then_inc(kc_ready, 1)

                if f:
                    for t in range(CC):
                        pe.wait_ge(hw_done, f.at(2, t + 1))
                        for j in range(HC):
                            last = nc.tensor.transpose(tp[:, t, j * P:(j + 1) * P], hw[:, t, j * P:(j + 1) * P],
                                                       ident[:, :])
                        last.then_inc(ht_ready, 1)
                for s in range(NT + Q_LAG):
                    if a and s < NT:
                        if s == 0:
                            if not f:
                                pe.wait_ge(w_lo, 4)
                            pe.wait_ge(z1_split, a.at(2, 2))
                        elif s == 1 and f:
                            pe.wait_ge(gate_read, f.at(1, 1))
                        elif s == 2:
                            pe.wait_ge(kc_split, a.at(2, 1))
                        elif s >= 3:
                            pe.wait_ge(q_exp, a.at(16, s - 2))
                        for c in range(CC):
                            last = mac3(ps[:, Q_RING[s % 3], :], opnd[:, HI, c, s * P:(s + 1) * P],
                                        opnd[:, LO, c, s * P:(s + 1) * P], wq[:, HI, c, :], wq[:, LO, c, :],
                                        c == 0, c == CC - 1)
                        last.then_inc(q_ready, 1)
                    if a and s == CX_AT:
                        pe.wait_ge(kc_split, a.at(2, 2))
                        for j in range(HC):
                            two = slice(j * P, (j + 1) * P)
                            for c in range(CC):
                                last = mac3(ps[:, M_BANK, two], wv[:, HI, c, two], wv[:, LO, c, two],
                                            kc[:, HI, c, two], kc[:, LO, c, two], c == 0, c == CC - 1)
                        last.then_inc(cx_ready, 1)
                    if a and s in MM_AT:
                        half = MM_AT.index(s)
                        if half:
                            pe.wait_ge(m_read, a.at(4, 2))
                        else:
                            pe.wait_ge(bd_split, a.at(1, 1))
                        for j in (2 * half, 2 * half + 1):
                            two = slice(j * P, (j + 1) * P)
                            last = mac3(ps[:, M_BANK, (j % 2) * DIM:(j % 2 + 1) * DIM],
                                        bd[:, HI, two], bd[:, LO, two], wo[:, HI, j, :], wo[:, LO, j, :], True, True)
                        last.then_inc(m_ready, 1)
                    if a and s >= Q_LAG:
                        i = s - Q_LAG
                        pe.wait_ge(q_nrm, a.at(16, i + 1))
                        if i >= 2:
                            pe.wait_ge(qt_done, a.at(16, i - 1))
                        elif f:
                            pe.wait_ge(ht_done, f.at(2, i + 1))
                        for j in range(HC):
                            last = nc.tensor.transpose(tp[:, i % 2, j * P:(j + 1) * P],
                                                       ke[:, i % 8, j * P:(j + 1) * P], ident[:, :])
                        last.then_inc(qt_ready, 1)
                    if f and Y_AT <= s < Y_AT + 16:
                        u, half = (s - Y_AT) // 2, (s - Y_AT) % 2
                        t, nb = u // NB, u % NB
                        if half == 0:
                            if nb == 0:
                                pe.wait_ge(ht_done, f.at(2, t + 1))
                            if u >= 2:
                                pe.wait_ge(fin_done, f.at(8, u - 1))
                        for j in (2 * half, 2 * half + 1):
                            last = mac3(ps[:, PAIR[u % 2], :], hwt[:, HI, j, t * P:(t + 1) * P],
                                        hwt[:, LO, j, t * P:(t + 1) * P], wb[:, HI, j, nb * 512:nb * 512 + 512],
                                        wb[:, LO, j, nb * 512:nb * 512 + 512], j == 0, j == HC - 1)
                        if half:
                            last.then_inc(y_ready, 1)

                    if a and s >= NT:
                        out_tile(a, f, s - NT)
                if not f:
                    pe.wait_ge(w_lo, W_PARTS)

                for i in range(Q_LAG, 8 if a else 0):
                    out_tile(a, f, i)

            turns(pe, body)


def kernel(x, ctx_4096, L0_xattn_Wq, L0_xattn_Wk, L0_xattn_Wv, L0_xattn_Wo, L0_xattn_bo, L0_xattn_g,
           L0_ffn_gate_w, L0_ffn_lora_A, L0_ffn_lora_B):
    import numpy as np
    import concourse.bacc as bacc
    from concourse import mybir as mb
    from concourse.bass_utils import run_bass_kernel_spmd

    def chunks(w):
        k, m = w.shape
        return np.ascontiguousarray(w.reshape(k // P, P, m).transpose(1, 0, 2).reshape(P, -1))

    arr = {k: np.asarray(v) for k, v in dict(
        x=x, ctx=ctx_4096, wq=L0_xattn_Wq, wk=L0_xattn_Wk, wv=L0_xattn_Wv, wo=L0_xattn_Wo, bo=L0_xattn_bo,
        g=L0_xattn_g, gate=L0_ffn_gate_w, la=L0_ffn_lora_A, lb=L0_ffn_lora_B).items()}
    n = arr["x"].shape[2]
    ins = {
        "x": np.ascontiguousarray(arr["x"]),
        "ctx": np.ascontiguousarray(arr["ctx"]),
        "wqT": chunks(arr["wq"].T), "wkT": chunks(arr["wk"].T), "wvT": chunks(arr["wv"].T),
        "woT": chunks(arr["wo"].T),
        "bo": np.ascontiguousarray(arr["bo"].reshape(-1, P).T),
        "g": np.ascontiguousarray(arr["g"].reshape(-1, P).T),
        "gateT": chunks(arr["gate"].T).reshape(P, n // P, E_N),
        "aT": chunks(arr["la"].reshape(-1, n).T),
        "bT": chunks(arr["lb"].transpose(0, 2, 1).reshape(-1, n)),
    }
    nc = bacc.Bacc("TRN2", target_bir_lowering=False, num_devices=1, dynamic_dma_scratch_size=1024)
    args = [nc.dram_tensor(f"in_{k}", a.shape, mb.dt.from_np(a.dtype), kind="ExternalInput").ap() for k, a in ins.items()]
    out = nc.dram_tensor("out_0", arr["x"].shape, mb.dt.float32, kind="ExternalOutput").ap()
    build(nc, *args, out)
    r = run_bass_kernel_spmd(nc, [{f"in_{k}": a for k, a in ins.items()}], core_ids=[0])
    return r.results[0]["out_0"]
```
